# Optimizing a Trainium2 kernel written in Bass

```python
import numpy as np
import jax
import jax.numpy as jnp

def _softmax(x, axis=-1):
    return jax.nn.softmax(x, axis=axis)

def _gelu(x):
    return jax.nn.gelu(x, approximate=True)

def _silu(x):
    return jax.nn.silu(x)

def _sigmoid(x):
    return jax.nn.sigmoid(x)

def _layernorm(x, axis=-1, eps=1e-05):
    m = jnp.mean(x, axis=axis, keepdims=True)
    v = jnp.var(x, axis=axis, keepdims=True)
    return (x - m) / jnp.sqrt(v + eps)

def _scatter_add(tgt, idx, src, axis=0):
    return tgt.at[idx].add(src)

def _segment_sum(src, seg, n):
    return jax.ops.segment_sum(src, seg, n)
kernel_name = 'mk_vit_tower_d1_tok_img768_r4_3a083f'

def setup_inputs(seed: int=0):
    np.random.seed(seed)
    _w = jnp.asarray

    def _rec_inputs():
        import jax
        import jax.numpy as jnp
        _rk = jax.random.key(seed)
        x = 7.57192e-06 + 1.00007 * jax.random.normal(jax.random.fold_in(_rk, 1), (32, 128, 128, 3), jnp.float32)
        return x
    x = _rec_inputs()

    def _L0_tok_setup():
        import jax, jax.numpy as jnp
        import numpy as np
        PATCH = 16
        DIM = 192
        EPS = 0.001

        def _shifts(x):
            zw = jnp.zeros_like(x[:, :, :1, :])
            right = jnp.concatenate([zw, x[:, :, :-1, :]], axis=2)
            left = jnp.concatenate([x[:, :, 1:, :], zw], axis=2)
            zh = jnp.zeros_like(x[:, :1, :, :])
            down = jnp.concatenate([zh, x[:, :-1, :, :]], axis=1)
            up = jnp.concatenate([x[:, 1:, :, :], zh], axis=1)
            return [right, left, down, up]

        def _patchify(x, p):
            b, H, W, C = x.shape
            hh, ww = (H // p, W // p)
            x = x.reshape(b, hh, p, ww, p, C)
            x = x.transpose(0, 1, 3, 2, 4, 5)
            return x.reshape(b, hh * ww, p * p * C)
        key = jax.random.key(seed)
        k1, k2 = jax.random.split(key)
        b, H, Wd, C = (64, 224, 224, 3)
        F = PATCH * PATCH * 5 * C
        x = jax.random.normal(k1, (b, H, Wd, C), dtype=jnp.float32)
        gamma = jnp.ones((F,), dtype=jnp.float32)
        beta = jnp.zeros((F,), dtype=jnp.float32)
        W = jax.random.normal(k2, (F, DIM), dtype=jnp.float32)
        bb = jnp.zeros((DIM,), dtype=jnp.float32)
        return {'x': x, 'gamma': gamma, 'beta': beta, 'W': W, 'b': bb}
    _L0_tok_all = _L0_tok_setup()
    _L0_tok_in = {k: v for k, v in _L0_tok_all.items() if k in ('gamma', 'beta', 'W', 'b')}
    del _L0_tok_all

    def _L0_attn_setup():
        import jax, jax.numpy as jnp
        import numpy as np
        B, N, C = (64, 80, 192)
        NUM_HEADS = 12
        LENS_Z = 64
        SCALE = (C // NUM_HEADS) ** (-0.5)
        key = jax.random.key(seed)
        k1, k2, k3 = jax.random.split(key, 3)
        x = jax.random.normal(k1, (B, N, C), dtype=jnp.float32)
        proj_w = jax.random.normal(k2, (C, C), dtype=jnp.float32) * 0.02
        proj_b = jax.random.normal(k3, (C,), dtype=jnp.float32) * 0.02
        return {'x': x, 'proj_w': proj_w, 'proj_b': proj_b}
    _L0_attn_all = _L0_attn_setup()
    _L0_attn_in = {k: v for k, v in _L0_attn_all.items() if k in ('proj_w', 'proj_b')}
    del _L0_attn_all

    def _L0_ffn_setup():
        import jax, jax.numpy as jnp
        import numpy as np
        D_MODEL = 192
        N_EXPERTS = 8
        TOP_K = 2
        D_FF = 4 * D_MODEL
        key = jax.random.key(seed)
        ks = jax.random.split(key, 6)
        B, S = (2, 512)
        x = jax.random.normal(ks[0], (B, S, D_MODEL), dtype=jnp.float32)
        Wr = jax.random.normal(ks[1], (D_MODEL, N_EXPERTS), dtype=jnp.float32) * 0.02
        W1 = jax.random.normal(ks[2], (N_EXPERTS, D_MODEL, D_FF), dtype=jnp.float32) * 0.02
        b1 = jnp.zeros((N_EXPERTS, D_FF), dtype=jnp.float32)
        W2 = jax.random.normal(ks[3], (N_EXPERTS, D_FF, D_MODEL), dtype=jnp.float32) * 0.02
        b2 = jnp.zeros((N_EXPERTS, D_MODEL), dtype=jnp.float32)
        return {'x': x, 'Wr': Wr, 'W1': W1, 'b1': b1, 'W2': W2, 'b2': b2}
    _L0_ffn_all = _L0_ffn_setup()
    _L0_ffn_in = {k: v for k, v in _L0_ffn_all.items() if k in ('Wr', 'W1', 'b1', 'W2', 'b2')}
    del _L0_ffn_all
    return {'x': x, 'L0_tok_gamma': _L0_tok_in['gamma'], 'L0_tok_beta': _L0_tok_in['beta'], 'L0_tok_W': _L0_tok_in['W'], 'L0_tok_b': _L0_tok_in['b'], 'L0_attn_proj_w': _L0_attn_in['proj_w'], 'L0_attn_proj_b': _L0_attn_in['proj_b'], 'L0_ffn_Wr': _L0_ffn_in['Wr'], 'L0_ffn_W1': _L0_ffn_in['W1'], 'L0_ffn_b1': _L0_ffn_in['b1'], 'L0_ffn_W2': _L0_ffn_in['W2'], 'L0_ffn_b2': _L0_ffn_in['b2']}

def reference(x, L0_tok_gamma, L0_tok_beta, L0_tok_W, L0_tok_b, L0_attn_proj_w, L0_attn_proj_b, L0_ffn_Wr, L0_ffn_W1, L0_ffn_b1, L0_ffn_W2, L0_ffn_b2):
    import jax
    import jax.numpy as jnp

    def _L0_tok_ref(x, gamma, beta, W, b):
        import jax, jax.numpy as jnp
        import numpy as np
        PATCH = 16
        DIM = 192
        EPS = 0.001

        def _shifts(x):
            zw = jnp.zeros_like(x[:, :, :1, :])
            right = jnp.concatenate([zw, x[:, :, :-1, :]], axis=2)
            left = jnp.concatenate([x[:, :, 1:, :], zw], axis=2)
            zh = jnp.zeros_like(x[:, :1, :, :])
            down = jnp.concatenate([zh, x[:, :-1, :, :]], axis=1)
            up = jnp.concatenate([x[:, 1:, :, :], zh], axis=1)
            return [right, left, down, up]

        def _patchify(x, p):
            b, H, W, C = x.shape
            hh, ww = (H // p, W // p)
            x = x.reshape(b, hh, p, ww, p, C)
            x = x.transpose(0, 1, 3, 2, 4, 5)
            return x.reshape(b, hh * ww, p * p * C)
        x5 = jnp.concatenate([x] + _shifts(x), axis=-1)
        tokens = _patchify(x5, PATCH)
        mu = jnp.mean(tokens, axis=-1, keepdims=True)
        var = jnp.mean(jnp.square(tokens - mu), axis=-1, keepdims=True)
        ln = (tokens - mu) * jax.lax.rsqrt(var + EPS) * gamma + beta
        return jnp.einsum('bnf,fd->bnd', ln, W) + b

    def _L0_attn_ref(x, proj_w, proj_b):
        import jax, jax.numpy as jnp
        import numpy as np
        B, N, C = (64, 80, 192)
        NUM_HEADS = 12
        LENS_Z = 64
        SCALE = (C // NUM_HEADS) ** (-0.5)
        q = x[:, :LENS_Z]
        k = x[:, LENS_Z:]
        v = k
        attn = jnp.einsum('bqc,bkc->bqk', q, k) * SCALE
        attn = jax.nn.softmax(attn, axis=-1)
        out = jnp.einsum('bqk,bkc->bqc', attn, v)
        out = jnp.transpose(out, (0, 2, 1)).reshape(out.shape[0], -1, C)
        out = out @ proj_w.T + proj_b
        return jnp.concatenate([out, k], axis=1)

    def _L0_ffn_ref(x, Wr, W1, b1, W2, b2):
        import jax, jax.numpy as jnp
        import numpy as np
        D_MODEL = 192
        N_EXPERTS = 8
        TOP_K = 2
        D_FF = 4 * D_MODEL
        B, S, D = x.shape
        T = B * S
        x_flat = x.reshape(T, D)
        gate_logits = x_flat @ Wr
        topw, topi = jax.lax.top_k(gate_logits, TOP_K)
        topw = jax.nn.softmax(topw, axis=-1)
        combine = jnp.zeros((T, N_EXPERTS), dtype=x.dtype)
        combine = combine.at[jnp.arange(T)[:, None], topi].add(topw)
        h = jax.nn.relu(jnp.einsum('td,edh->eth', x_flat, W1) + b1[:, None, :])
        y = jnp.einsum('eth,ehd->etd', h, W2) + b2[:, None, :]
        out = jnp.einsum('te,etd->td', combine, y)
        return out.reshape(B, S, D)
    h = _L0_tok_ref(x, L0_tok_gamma, L0_tok_beta, L0_tok_W, L0_tok_b)
    h = h + _L0_attn_ref(_layernorm(h, axis=-1), L0_attn_proj_w, L0_attn_proj_b)
    h = h + _L0_ffn_ref(_layernorm(h, axis=-1), L0_ffn_Wr, L0_ffn_W1, L0_ffn_b1, L0_ffn_W2, L0_ffn_b2)
    return h

_drawn_inputs = setup_inputs


def setup_inputs(seed=0):
    import zlib

    import numpy as np

    out = dict(_drawn_inputs(seed))
    spreads = {'L0_tok_gamma': (1.0, 0.2),
     'L0_tok_beta': (0.0, 0.1),
     'L0_tok_b': (0.0, 2.0),
     'L0_ffn_b1': (0.0, 0.8),
     'L0_ffn_b2': (0.0, 2.0)}
    factors = {'L0_attn_proj_b': 172.179, 'L0_ffn_Wr': 8.0, 'L0_ffn_W1': 8.0, 'L0_ffn_W2': 8.0}
    for name, (base, spread) in spreads.items():
        noise = np.random.default_rng([zlib.crc32(name.encode()), seed]).standard_normal(out[name].shape)
        drawn = base * np.exp(spread * noise) if base else spread * noise
        out[name] = jnp.asarray(drawn.astype(out[name].dtype))
    for name, factor in factors.items():
        out[name] = (out[name] * factor).astype(out[name].dtype)
    return out
```

```python
from contextlib import ExitStack

import numpy as np
import concourse.bass as bass
from concourse import mybir

ALU = mybir.AluOpType
ACT = mybir.ActivationFunctionType
AX = mybir.AxisListType
F32 = mybir.dt.float32
F32R = mybir.dt.float32r
BF16 = mybir.dt.bfloat16
I32 = mybir.dt.int32
U32 = mybir.dt.uint32

P = 128
IMAGES, SIDE, CH = 32, 128, 3
PATCH = 16
GRID = SIDE // PATCH
SHIFTS = 5
D = 192
N_TOK = IMAGES * GRID * GRID
FEAT = PATCH * PATCH * SHIFTS * CH
CORE = PATCH * PATCH * CH
HALO = 4 * PATCH * CH
CORE_CH = CORE // P
KCH = CORE_CH + 2
HALO_B = HALO - P
N_W = CORE_CH * SHIFTS + 2
TILES = N_TOK // P
GT = 2
GROUPS = TILES // GT
EPS_TOK, EPS_LN = 1e-3, 1e-5
NE, TOPK = 8, 2
FF = 4 * D
FCH = FF // P
HA = 512
D2 = D - P
ROW = 4 * P
SLOT_TILES = TOPK * N_TOK // P + NE - 1
UNROLL = 3
assert SLOT_TILES % UNROLL == 0
LATE = 2
PC = 256
BIG = 3e38


def feature_maps():
    def feat(i, j, s, c):
        return (i * PATCH + j) * SHIFTS * CH + s * CH + c

    core = np.full((CORE, SHIFTS), FEAT)
    for i in range(PATCH):
        for j in range(PATCH):
            shown = ((i, j), (i, j + 1), (i, j - 1), (i + 1, j), (i - 1, j))
            for s, (a, b) in enumerate(shown):
                if 0 <= a < PATCH and 0 <= b < PATCH:
                    for c in range(CH):
                        core[(i * PATCH + j) * CH + c, s] = feat(a, b, s, c)
    last = PATCH - 1
    sides = [[feat(i, 0, 1, c) for i in range(PATCH) for c in range(CH)],
             [feat(i, last, 2, c) for i in range(PATCH) for c in range(CH)],
             [feat(0, j, 3, c) for j in range(PATCH) for c in range(CH)],
             [feat(last, j, 4, c) for j in range(PATCH) for c in range(CH)]]
    halo = np.concatenate(sides)
    count = np.concatenate([(core < FEAT).sum(1), np.ones(HALO), np.zeros(P - HALO_B)])
    return core, halo, count.reshape(KCH, P).T.astype(np.float32)


def by_slab(w):
    core, halo, _ = feature_maps()
    padded = np.concatenate([w, np.zeros((1, w.shape[1]), w.dtype)])
    return padded[core].reshape(CORE_CH, P, SHIFTS, -1), w[halo]



def vit_tower_kernel(nc, pix_a, pix_b, w_core, w_halo, gb, count, sel, bias2, proj_t, wr, w1, b1, w2,
                     b2, out):
    ctx = ExitStack()
    with ctx:
        def sem(name):
            return ctx.enter_context(nc.semaphore(name))

        def sb(name, shape, dt=F32, stack=ctx):
            return stack.enter_context(nc.sbuf_tensor(name, shape, dt))

        xrow_d = nc.dram_tensor("xrow_d", [N_TOK, ROW], F32)
        resid_d = nc.dram_tensor("resid_d", [N_TOK, D], F32)
        y_d = nc.dram_tensor("y_d", [TOPK * N_TOK + SLOT_TILES * P, D], F32)

        fin = ExitStack()
        res_f = sb("res_f", [P, TILES, D], stack=fin)
        y0_f = sb("y0_f", [P, TILES, D], stack=fin)
        y1_f = sb("y1_f", [P, TILES, D], stack=fin)
        fin.close()
        w1_hi = sb("w1_hi", [P, NE, FF], F32R)
        w1_lo = sb("w1_lo", [P, NE, FF], F32R)
        w1_2 = sb("w1_2", [P, NE, FF], F32R)
        setup = ExitStack()
        w5 = sb("w5", [P, CORE_CH, SHIFTS, D], stack=setup)
        w5h = sb("w5h", [P, 2, D], stack=setup)
        setup.close()
        w1_b = sb("w1_b", [P, NE, FF], F32R)
        pixels = ExitStack()
        sb("w2s_first", [P, NE - LATE, 2, FCH, D], F32R, stack=pixels)
        xbuf = sb("xbuf", [P, 4, KCH, P], stack=pixels)
        attn = sb("attn", [P, P], stack=pixels)
        proj_s = sb("proj_s", [P, 2, D], stack=pixels)
        pixels.close()
        w2s = sb("w2s", [P, NE, 2, FCH, D], F32R)

        identr = sb("identr", [P, P], F32R)
        xts = [sb(f"xts{k}", [P, ROW], F32R)[:] for k in range(GT)]
        logits = sb("logits", [P, TILES, NE])
        wgt = sb("wgt", [P, TOPK, TILES])
        tab = sb("tab", [P, 2, SLOT_TILES + UNROLL], I32)
        etab = sb("etab", [1, SLOT_TILES + 1], I32)
        tri = sb("tri", [P, P], BF16)
        onesb = sb("onesb", [P, P], BF16)
        row128 = sb("row128", [P, P], BF16)
        tile_no = sb("tile_no", [P, SLOT_TILES + 1])
        pad_row = sb("pad_row", [P, SLOT_TILES])
        first_e = sb("first_e", [P, NE])
        block_no = sb("block_no", [P, TOPK * TILES])
        p_plus1 = sb("p_plus1", [P, 1])
        restart = sb("restart", [P, NE, TILES])
        raws = ExitStack()
        raw_a = sb("raw_a", [P, FF], stack=raws)
        raw_b = sb("raw_b", [P, FF], stack=raws)
        raw_2 = sb("raw_2", [P, FCH, D], stack=raws)
        raws.close()
        h_hi = sb("h_hi", [P, FF], F32R)
        h_lo = sb("h_lo", [P, FF], F32R)
        ht_hi = sb("ht_hi", [P, FCH, P], F32R)
        sb("rest_of_raw_2", [P, FCH * D - FF])

        emb = ExitStack()
        wt = sb("wt", [P, KCH, D + 2], stack=emb)
        gb_s = sb("gb_s", [P, N_W, 2], stack=emb)
        cnt_s = sb("cnt_s", [P, KCH], stack=emb)
        cb = sb("cb", [P, 2, D], stack=emb)
        rows = sb("rows", [P, 2, GT, ROW], F32R, stack=emb)
        first = ExitStack()
        sel_s = sb("sel_s", [2, 3, P], stack=first)
        bias2_s = sb("bias2_s", [2, D], stack=first)
        cb_row = sb("cb_row", [2, D], stack=first)
        ident = sb("ident", [P, P], stack=first)
        ints = sb("ints", [P, P], I32, stack=first)
        first.close()
        h = sb("h", [P, 2, GT, D], stack=emb)
        xn = sb("xn", [P, GT, D], stack=emb)
        u = xn
        small = sb("small", [P, 8, GT], stack=emb)
        bst = sb("bst", [P, GT, 6], stack=emb)
        mv = sb("mv", [P, GT, 2], stack=emb)
        minus_half = sb("minus_half", [P, GT], stack=emb)
        wr_raw = sb("wr_raw", [P, 2, NE], stack=emb)
        wr_hi = sb("wr_hi", [P, NE], F32R, stack=emb)
        wr_lo = sb("wr_lo", [P, NE], F32R, stack=emb)
        wr_2h = sb("wr_2h", [P, NE], F32R, stack=emb)
        wr_2 = sb("wr_2", [P, NE], F32R, stack=emb)
        emb.close()

        disp = ExitStack()
        oh = sb("oh", [P, TOPK, NE, TILES], stack=disp)
        eq = sb("eq", [P, TILES, NE], stack=disp)
        l2 = sb("l2", [P, TILES, NE], stack=disp)
        top = sb("top", [P, TOPK, TILES], stack=disp)
        found = sb("found", [P, TOPK, TILES], stack=disp)
        chosen = sb("chosen", [P, NE, TILES], BF16, stack=disp)
        tot = sb("tot", [P, NE, TILES], stack=disp)
        incl = sb("incl", [P, NE, TILES], stack=disp)
        base = sb("base", [P, NE, TILES], stack=disp)
        spare = raw_2[:].rearrange("p c d -> p (c d)")
        picked = spare[:, 0:TOPK * NE * TILES].rearrange("p (k e t) -> p k e t", k=TOPK, e=NE)
        after = TOPK * NE * TILES
        e_cmp = spare[0:1, after:after + (SLOT_TILES + 1) * NE].rearrange("p (a e) -> p a e", e=NE)
        e_int = sb("e_int", [P, NE], I32, stack=disp)
        e_til = sb("e_til", [P, NE], stack=disp)
        e_end = sb("e_end", [P, NE], stack=disp)
        e_one = sb("e_one", [P, NE], stack=disp)
        slot = sb("slot", [P, TOPK * TILES], I32, stack=disp)
        slot_i = sb("slot_i", [P, 2, TOPK * TILES], I32, stack=disp)
        slot_f = sb("slot_f", [P, 2, TOPK * TILES], stack=disp)
        part = sb("part", [P, TOPK * TILES, 2, SLOT_TILES], BF16, stack=disp)
        in_tile = sb("in_tile", [P, TOPK * TILES, SLOT_TILES], BF16, stack=disp)
        in_row = sb("in_row", [P, TOPK * TILES, P], BF16, stack=disp)
        ts = sb("ts", [P, 2, SLOT_TILES], stack=disp)
        code = sb("code", [P, 3, SLOT_TILES], stack=disp)
        code_i = sb("code_i", [P, SLOT_TILES], I32, stack=disp)
        e_sum = sb("e_sum", [1, SLOT_TILES + 1], stack=disp)
        wex = sb("wex", [P, 3, TILES], stack=disp)
        disp.close()

        b1_s, b1_hi = raw_a[0:NE], raw_b[0:NE]

        xts.append(sb("xts2", [P, ROW], F32R)[:])
        b2_s = sb("b2_s", [P, NE, D])
        gath = sb("gath", [P, UNROLL, ROW], F32R)
        ht_lo = sb("ht_lo", [P, FCH, P], F32R)
        y_s = sb("y_s", [P, UNROLL, D])
        idx = sb("idx", [P, 2, 2, UNROLL], U32)

        bank = [ctx.enter_context(nc.psum_tensor(f"bank{n}", [P, 512], F32)) for n in range(8)]
        p_tok = bank[0:2]
        p_xt = [bank[2], bank[3]]
        p_lg, p_set, p_bc, p_disp = bank[4], bank[5], bank[6], bank[7]
        p_ha, p_hb, p_hia, p_hib, p_loa, p_lob, p_y, p_x = bank

        s_gb, s_small, s_b2, s_b1 = sem("s_gb"), sem("s_small"), sem("s_b2"), sem("s_b1")
        s_w5 = [sem(f"s_w5_{c}") for c in range(CORE_CH + 1)]
        x_loaded = [sem(f"x_loaded{b}") for b in range(4)]
        raw_a_loaded, raw_b_loaded, raw_2_loaded = sem("raw_a_loaded"), sem("raw_b_loaded"), sem("raw_2_loaded")
        consts = sem("consts")
        row_sums = sem("row_sums")
        row_copied = sem("row_copied")
        bc_ready = sem("bc_ready")
        dset = sem("dset")
        x_used = sem("x_used")
        sq_ready = sem("sq_ready")
        sq_used = sem("sq_used")
        p_free = sem("p_free")
        step = sem("step")
        var_tok, rstd_tok = sem("var_tok"), sem("rstd_tok")
        var_ln, rstd_ln = sem("var_ln"), sem("rstd_ln")
        xn_ready, row_hi, row_lo = sem("xn_ready"), sem("row_hi"), sem("row_lo")
        xt_ready, xts_ready = sem("xt_ready"), sem("xts_ready")
        lg_ready, lg_copied = sem("lg_ready"), sem("lg_copied")
        rows_stored = [sem(f"rows_stored{k}") for k in range(2)]
        hi_a, hi_b, lo_a, lo_b = sem("hi_a"), sem("hi_b"), sem("lo_a"), sem("lo_b")
        hi_2, lo_2 = sem("hi_2"), sem("lo_2")
        ds = sem("ds")
        chosen_ready, counts_ready = sem("chosen_ready"), sem("counts_ready")
        top_ready, exp_ready = sem("top_ready"), sem("exp_ready")
        hot_ready, tab_sums = sem("hot_ready"), sem("tab_sums")
        tab_ready, etab_ready = sem("tab_ready"), sem("etab_ready")
        b1_placed = sem("b1_placed")
        g_loaded = [sem(f"g_loaded{k}") for k in range(UNROLL)]
        idx_staged = sem("idx_staged")
        gx_ready, gxs_ready = sem("gx_ready"), sem("gxs_ready")
        ha_ready, hb_ready = sem("ha_ready"), sem("hb_ready")
        relu_hi, relu_lo = sem("relu_hi"), sem("relu_lo")
        thi_ready, tlo_ready = sem("thi_ready"), sem("tlo_ready")
        thi_copied, tlo_copied = sem("thi_copied"), sem("tlo_copied")
        y_ready, y_copied = sem("y_ready"), sem("y_copied")
        y_stored = [sem(f"y_stored{k}") for k in range(UNROLL)]
        res_loaded = sem("res_loaded")
        FIN = 4
        y_loaded = [sem(f"y_loaded{c}") for c in range(FIN)]
        mixed, out_ready, stored = sem("mixed"), sem("out_ready"), sem("stored")
        int_made, hi_r, wr_split, cb_ready = sem("int_made"), sem("hi_r"), sem("wr_split"), sem("cb_ready")
        b1_half, wgt_ready = sem("b1_half"), sem("wgt_ready")
        N_CONST = 12
        N_SET = 5 * CORE_CH + 3
        STEPS = 10

        block = ctx.enter_context(nc.Block())

        def early(g, n):
            return isinstance(g, int) and g < n

        def groups(eng, group):
            for g in range(2):
                group(g, g)
            with eng.Fori(2, GROUPS - 1, 2) as i:
                for par in range(2):
                    group(i + par, par)

        @block.sync
        def _(sp):
            sp.dma_start(gb_s[:], gb).then_inc(s_gb, 16)
            for c in range(CORE_CH):
                sp.dma_start(w5[:, c], w_core[c]).then_inc(s_w5[c], 16)
            sp.dma_start(w5h[:, 0], w_halo[0:P]).then_inc(s_w5[CORE_CH], 16)
            sp.dma_start(w5h[0:HALO_B, 1], w_halo[P:HALO]).then_inc(s_w5[CORE_CH], 16)
            sp.dma_start(cnt_s[:], count).then_inc(s_small, 16)
            sp.dma_start(sel_s[:], sel).then_inc(s_small, 16)
            sp.dma_start(bias2_s[:], bias2).then_inc(s_small, 16)
            sp.dma_start(proj_s[:, 0], proj_t[0:P]).then_inc(s_small, 16)
            sp.dma_start(proj_s[0:D2, 1], proj_t[P:D]).then_inc(s_small, 16)
            sp.dma_start(wr_raw[:, 0], wr[0:P]).then_inc(s_small, 16)
            sp.dma_start(wr_raw[0:D2, 1], wr[P:D]).then_inc(s_small, 16)
            sp.dma_start(wr_raw[D2:P, 1], wr[P:D]).then_inc(s_small, 16)

            def group(g, par):
                for k in range(GT):
                    t, b = GT * g + k, GT * par + k
                    if not early(g, 2):
                        sp.wait_ge(sq_used, t - 3)
                    sp.dma_start(xbuf[:, b, 0:KCH - 1], pix_a[bass.ds(t, 1)].rearrange("o p k t -> p (o k) t"))\
                        .then_inc(x_loaded[b], 16)
                    sp.dma_start(xbuf[0:HALO_B, b, KCH - 1], pix_b[bass.ds(t, 1)].rearrange("o p t -> p (o t)"))\
                        .then_inc(x_loaded[b], 16)
                if not early(g, 1):
                    sp.wait_ge(lo_a, g)
                sp.dma_start(raw_a[:], w1[bass.ds(g, 1), 0:P].rearrange("e p f -> p (e f)")).then_inc(raw_a_loaded, 16)
                if not early(g, 1):
                    sp.wait_ge(lo_b, g)
                for lo in (0, D2):
                    sp.dma_start(raw_b[lo:lo + D2], w1[bass.ds(g, 1), P:D].rearrange("e p f -> p (e f)"))\
                        .then_inc(raw_b_loaded, 16)
                if not early(g, 2):
                    sp.wait_ge(lo_2, g - 1)
                    sp.dma_start(raw_2[:], w2[bass.ds(g - 2, 1)].rearrange("e (c p) d -> p (e c) d", p=P))\
                        .then_inc(raw_2_loaded, 16)

            groups(sp, group)
            for e in range(NE - LATE, NE):
                sp.wait_ge(lo_2, e + 1)
                sp.dma_start(raw_2[:], w2[e].rearrange("(c p) d -> p c d", p=P)).then_inc(raw_2_loaded, 16)
            sp.wait_ge(lo_a, NE)
            sp.wait_ge(lo_b, NE)
            sp.dma_start(b1_s, b1).then_inc(s_b1, 16)
            sp.wait_ge(b1_placed, 2)
            sp.dma_start(w1_b[D2:D2 + 1].bitcast(F32), b1_hi).then_inc(b1_placed, 16)
            sp.dma_start(w1_b[D2 + 1:D2 + 2].bitcast(F32), b1_s).then_inc(b1_placed, 16)
            sp.wait_ge(tab_ready, 2)
            sp.wait_ge(etab_ready, 1)
            sp.wait_ge(b1_placed, 34)
            sp.dma_start(b2_s[:].rearrange("p e d -> p (e d)"),
                         b2.rearrange("(o e) d -> o (e d)", o=1).to_broadcast((P, NE * D))).then_inc(s_b2, 16)
            sp.wait_ge(hb_ready, SLOT_TILES)
            for k in range(2):
                sp.wait_ge(rows_stored[k], 32 * GROUPS // 2)
            sp.dma_start(res_f[:], resid_d[:].rearrange("(t p) d -> p t d", p=P)).then_inc(res_loaded, 16)
            for k in range(UNROLL):
                sp.wait_ge(y_stored[k], 16 * (SLOT_TILES // UNROLL))
            n = TILES // FIN
            for c in range(FIN):
                for k, buf in enumerate((y0_f, y1_f)):
                    at = k * N_TOK + c * n * P
                    sp.dma_start(buf[:, c * n:(c + 1) * n],
                                 y_d[at:at + n * P].rearrange("(t p) d -> p t d", p=P)).then_inc(y_loaded[c], 16)
            for c in range(FIN):
                sp.wait_ge(out_ready, c + 1)
                sp.dma_start(out[c * n * P:(c + 1) * n * P].rearrange("(t p) d -> p t d", p=P),
                             res_f[:, c * n:(c + 1) * n]).then_inc(stored, 16)
            sp.wait_ge(stored, 16 * FIN)

        @block.gpsimd
        def _(pool):
            g_ = nc.gpsimd
            g_.memset(ident[:], 1.0).then_inc(consts, 1)
            g_.memset(tri[:], 1.0).then_inc(consts, 1)
            g_.memset(onesb[:], 1.0).then_inc(consts, 1)
            g_.memset(minus_half[:], -0.5).then_inc(consts, 1)
            g_.memset(rows[:].bitcast(F32), 0.0).then_inc(consts, 1)
            g_.memset(restart[:], 1.0).then_inc(consts, 1)
            pool.wait_ge(consts, 6)
            g_.affine_select(out=ident[:], in_=ident[:], compare_op=ALU.is_equal, fill=0.0, base=0,
                             pattern=[[-1, P]], channel_multiplier=1).then_inc(consts, 1)
            g_.affine_select(out=tri[:], in_=tri[:], compare_op=ALU.is_gt, fill=0.0, base=0,
                             pattern=[[1, P]], channel_multiplier=-1).then_inc(consts, 1)
            g_.memset(rows[:, :, :, ROW - D2:ROW - D2 + 2].bitcast(F32), 1.0).then_inc(consts, 1)
            g_.memset(restart[:, :, 0:1], 0.0).then_inc(consts, 1)

            def floats(out_, n, pattern, base_, cm):
                g_.iota(ints[:, 0:n], pattern=pattern, base=base_, channel_multiplier=cm).then_inc(int_made, 1)
                made[0] += 1
                pool.wait_ge(int_made, made[0])
                g_.tensor_copy(out_, ints[:, 0:n]).then_inc(int_made, 1)
                made[0] += 1
                pool.wait_ge(int_made, made[0])

            made = [0]
            floats(first_e[:], NE, [[-1, NE]], NE, 0)
            floats(row128[:], P, [[1, P]], 0, 0)
            floats(tile_no[:], SLOT_TILES + 1, [[1, SLOT_TILES + 1]], 0, 0)
            floats(pad_row[:], SLOT_TILES, [[P, SLOT_TILES]], TOPK * N_TOK + 1, 1)
            floats(block_no[:], TOPK * TILES, [[1, TOPK * TILES]], 0, 0)
            floats(p_plus1[:], 1, [[0, 1]], 1, 1)
            g_.memset(attn[:], 0.0).then_inc(consts, 1)
            g_.memset(tab[:, 1, 0:UNROLL], 0).then_inc(consts, 1)

            def group(g, par):
                if not early(g, 1):
                    pool.wait_ge(lo_a, g)
                pool.wait_ge(var_tok, g + 1)
                g_.tensor_tensor(small[:, 4], small[:, 3], minus_half[:], ALU.pow).then_inc(rstd_tok, 1)
                pool.wait_ge(var_ln, g + 1)
                g_.tensor_tensor(small[:, 6], small[:, 5], minus_half[:], ALU.pow).then_inc(rstd_ln, 1)
                pool.wait_ge(hi_a, g + 1)
                pool.wait_ge(hi_b, g + 1)
                pool.wait_ge(rstd_ln, g + 1)
                pool.nop(nofuse=True)
                g_.tensor_tensor(w1_2[D2:P, bass.ds(g, 1)].rearrange("p e f -> p (e f)"), raw_b[D2:P],
                                 w1_b[D2:P, bass.ds(g, 1)].rearrange("p e f -> p (e f)").bitcast(F32),
                                 ALU.subtract).then_inc(lo_b, 1)
                pool.wait_ge(lo_b, g + 1)
                pool.nop(nofuse=True)
                g_.tensor_tensor(w1_lo[:, bass.ds(g, 1)].rearrange("p e f -> p (e f)"), raw_a[:],
                                 w1_hi[:, bass.ds(g, 1)].rearrange("p e f -> p (e f)").bitcast(F32),
                                 ALU.subtract).then_inc(lo_a, 1)

            groups(pool, group)

            def gather(k, ix):
                g_.indirect_dma_start(out=gath[:, k].bitcast(F32), out_offset=None, in_=xrow_d[:],
                                      in_offset=bass.IndirectOffsetOnAxis(ap=ix, axis=0)).then_inc(g_loaded[k], 16)

            def scatter(k, ix):
                g_.indirect_dma_start(out=y_d[:], out_offset=bass.IndirectOffsetOnAxis(ap=ix, axis=0),
                                      in_=y_s[:, k], in_offset=None).then_inc(y_stored[k], 16)

            pool.wait_ge(tab_ready, 2)
            pool.wait_ge(etab_ready, 1)
            pool.wait_ge(b1_placed, 34)
            for k in range(2):
                pool.wait_ge(rows_stored[k], 32 * GROUPS // 2)
            for k in range(UNROLL):
                gather(k, tab[:, 0, k:k + 1].bitcast(U32))

            def turn(j, par):
                g_.tensor_copy(idx[:, par].bitcast(I32), tab[:, :, bass.ds(j + UNROLL, UNROLL)]).then_inc(idx_staged, 1)
                for k in range(UNROLL):
                    pool.wait_ge(gx_ready, j + k + 1)
                    if k == 0:
                        pool.wait_ge(idx_staged, (j + UNROLL) // UNROLL if isinstance(j, int) else j // UNROLL + 1)
                    pool.nop(nofuse=True)
                    gather(k, idx[:, par, 0, k:k + 1])
                    pool.wait_ge(y_copied, j + k + 1)
                    pool.nop(nofuse=True)
                    scatter(k, idx[:, par, 1, k:k + 1])

            with pool.Fori(0, SLOT_TILES - 3 * UNROLL + 1, 2 * UNROLL) as i:
                for par in range(2):
                    turn(i + par * UNROLL, par)
            for k in range(UNROLL):
                j = SLOT_TILES - UNROLL + k
                pool.wait_ge(y_copied, j + 1)
                scatter(k, tab[:, 1, j + UNROLL:j + UNROLL + 1].bitcast(U32))

        @block.scalar
        def _(act):
            a_ = nc.scalar
            act.wait_ge(consts, N_CONST)
            a_.copy(identr[:], ident[:]).then_inc(hi_r, 1)
            act.wait_ge(s_small, 16 * 8)
            a_.copy(wr_hi[:], wr_raw[:, 0]).then_inc(hi_r, 1)
            a_.copy(wr_2h[:], wr_raw[:, 1]).then_inc(hi_r, 1)
            a_.copy(wr_2[0:D2], wr_raw[0:D2, 1]).then_inc(hi_r, 1)

            def square(t, b):
                act.wait_ge(x_used, t + 1)
                a_.activation(xbuf[:, b], xbuf[:, b], ACT.Square).then_inc(sq_ready, 1)

            def flat(w, e):
                return w[:, bass.ds(e, 1)].rearrange("p e f -> p (e f)")

            def split_2(e):
                a_.copy(w2s[:, bass.ds(e, 1), 0].rearrange("p e c d -> p (e c) d"), raw_2[:]).then_inc(hi_2, 1)

            def high_rows(g, par):
                act.wait_ge(xn_ready, GT * g + GT)
                a_.copy(rows[:, par, :, 0:D], xn[:])
                a_.copy(rows[:, par, :, D:D + D2], xn[:, :, P:D]).then_inc(row_hi, 1)

            def finish(g, par):
                for k in range(GT):
                    act.wait_ge(xt_ready, GT * g + k + 1)
                    a_.copy(xts[k], p_xt[k][:]).then_inc(xts_ready, 1)
                act.wait_ge(row_lo, g + 1)
                act.dma_start(xrow_d[:].rearrange("(t p) c -> p t c", p=P)[:, bass.ds(GT * g, GT)],
                              rows[:, par].bitcast(F32))\
                    .then_inc(rows_stored[par], 16)
                act.dma_start(resid_d[:].rearrange("(t p) c -> p t c", p=P)[:, bass.ds(GT * g, GT)], h[:, par])\
                    .then_inc(rows_stored[par], 16)

            def group(g, par):
                if not early(g, 1):
                    square(GT * g - 1, (GT * par - 1) % 4)
                act.wait_ge(raw_a_loaded, 16 * g + 16)
                act.wait_ge(raw_b_loaded, 32 * g + 32)
                if not early(g, 2):
                    act.wait_ge(raw_2_loaded, 16 * g - 16)
                act.wait_ge(row_sums, 1)
                act.wait_ge(dset, N_SET)
                a_.copy(flat(w1_hi, g), raw_a[:]).then_inc(hi_a, 1)
                a_.copy(flat(w1_b, g), raw_b[:])
                a_.copy(flat(w1_2[0:D2], g), raw_b[0:D2]).then_inc(hi_b, 1)
                if not early(g, 2):
                    split_2(g - 2)
                square(GT * g, GT * par)
                if not early(g, 2):
                    finish(g - 2, par)
                if not early(g, 1):
                    high_rows(g - 1, 1 - par)

            groups(act, group)
            square(TILES - 1, 3)
            finish(GROUPS - 2, 0)
            high_rows(GROUPS - 1, 1)
            for e in range(NE - LATE, NE):
                act.wait_ge(raw_2_loaded, 16 * e + 16)
                act.wait_ge(x_used, TILES)
                split_2(e)
                if e == NE - LATE:
                    finish(GROUPS - 1, 1)
            act.wait_ge(s_b1, 16)
            a_.copy(b1_hi.bitcast(F32R), b1_s).then_inc(b1_half, 1)
            act.wait_ge(top_ready, 1)
            a_.activation(wex[:, 1], wex[:, 0], ACT.Exp).then_inc(exp_ready, 1)

            def rows_t(j, k):
                act.wait_ge(gx_ready, j + 1)
                a_.copy(xts[k], p_x[:]).then_inc(gxs_ready, 1)

            def relu(j):
                act.wait_ge(ha_ready, j + 1)
                a_.activation(h_hi[:, 0:HA], p_ha[:], ACT.Relu).then_inc(relu_hi, 1)
                act.wait_ge(hb_ready, j + 1)
                a_.activation(h_hi[:, HA:FF], p_hb[:, 0:FF - HA], ACT.Relu).then_inc(relu_hi, 1)

            def tile(j, k, more, more2):
                act.wait_ge(thi_ready, 2 * j + 1)
                a_.copy(ht_hi[:, 0:4], p_hia[:].rearrange("p (c t) -> p c t", t=P)).then_inc(thi_copied, 1)
                act.wait_ge(thi_ready, 2 * j + 2)
                a_.copy(ht_hi[:, 4:6], p_hib[:, 0:2 * P].rearrange("p (c t) -> p c t", t=P)).then_inc(thi_copied, 1)
                if more:
                    relu(j + 1)
                if more2:
                    rows_t(j + 2, (k + 2) % UNROLL)

            rows_t(0, 0)
            rows_t(1, 1)
            relu(0)
            with act.Fori(0, SLOT_TILES - 2 * UNROLL + 1, UNROLL) as i:
                for k in range(UNROLL):
                    tile(i + k, k, True, True)
            for k in range(UNROLL):
                tile(SLOT_TILES - UNROLL + k, k, k < 2, k < 1)

        @block.vector
        def _(dve):
            v_ = nc.vector
            v_.memset(xbuf[D2:P, :, KCH - 1], 0.0).then_inc(lg_copied, 1)
            v_.memset(small[:], 1.0).then_inc(lo_2, 1)
            dve.wait_ge(s_gb, 16)
            n = 0
            for c in range(CORE_CH):
                dve.wait_ge(s_w5[c], 16)
                for s in range(SHIFTS):
                    g1 = gb_s[:, c * SHIFTS + s, 0:1]
                    if s == 0:
                        v_.tensor_scalar(wt[:, c, 0:D], w5[:, c, s], g1, None, ALU.mult).then_inc(dset, 1)
                    else:
                        dve.wait_ge(dset, n)
                        v_.scalar_tensor_tensor(out=wt[:, c, 0:D], in0=w5[:, c, s], scalar=g1, in1=wt[:, c, 0:D],
                                                op0=ALU.mult, op1=ALU.add).then_inc(dset, 1)
                    n += 1
            dve.wait_ge(s_w5[CORE_CH], 32)
            for k, rows_ in enumerate((P, HALO_B)):
                v_.tensor_scalar(wt[0:rows_, CORE_CH + k, 0:D], w5h[0:rows_, k],
                                 gb_s[0:rows_, CORE_CH * SHIFTS + k, 0:1], None, ALU.mult).then_inc(dset, 1)
            dve.wait_ge(s_small, 16 * 8)
            v_.tensor_copy(wt[:, :, D], cnt_s[:]).then_inc(dset, 1)
            dve.wait_ge(row_sums, 1)
            v_.tensor_copy(cb_row[:], p_set[0:2, 0:D]).then_inc(row_copied, 1)
            dve.wait_ge(hi_r, 4)
            v_.tensor_tensor(wr_lo[:], wr_raw[:, 0], wr_hi[:].bitcast(F32), ALU.subtract)
            v_.tensor_tensor(wr_2[D2:P], wr_raw[D2:P, 1], wr_2h[D2:P].bitcast(F32), ALU.subtract).then_inc(wr_split, 1)
            dve.wait_ge(bc_ready, 1)
            v_.tensor_copy(cb[:], p_bc[:, 0:2 * D].rearrange("p (n d) -> p n d", n=2)).then_inc(cb_ready, 1)
            dve.wait_ge(cb_ready, 1)

            def copy_logits(g):
                dve.wait_ge(lg_ready, g + 1)
                v_.tensor_scalar(logits[:, bass.ds(GT * g, GT)], p_lg[:, 0:GT * NE].rearrange("p (t e) -> p t e", t=GT),
                                 1.0, None, ALU.mult).then_inc(lg_copied, 1)

            def low_2(e):
                dve.wait_ge(hi_2, e + 1)
                v_.tensor_tensor(w2s[:, bass.ds(e, 1), 1].rearrange("p e c d -> p (e c) d"), raw_2[:],
                                 w2s[:, bass.ds(e, 1), 0].rearrange("p e c d -> p (e c) d").bitcast(F32),
                                 ALU.subtract).then_inc(lo_2, 1)

            def group(g, par):
                s0 = STEPS * g
                tok = p_tok[par][:].rearrange("p (k c) -> p k c", k=GT)
                nmu, a, mu2, var, rstd, vln, rln = (small[:, n] for n in range(7))
                dve.wait_ge(sq_used, GT * g + GT)
                v_.tensor_scalar(nmu, tok[:, :, D], -1.0 / FEAT, None, ALU.mult).then_inc(step, 1)
                v_.tensor_scalar(a, tok[:, :, D + 1], 1.0 / FEAT, EPS_TOK, ALU.mult, ALU.add).then_inc(step, 1)
                dve.wait_ge(step, s0 + 1)
                v_.tensor_tensor(mu2, nmu, nmu, ALU.mult).then_inc(step, 1)
                dve.wait_ge(step, s0 + 3)
                v_.tensor_tensor(var, a, mu2, ALU.subtract).then_inc(var_tok, 1)
                for k in range(GT):
                    v_.scalar_tensor_tensor(out=u[:, k], in0=cb[:, 0], scalar=nmu[:, k:k + 1], in1=tok[:, k, 0:D],
                                            op0=ALU.mult, op1=ALU.add).then_inc(step if k == 0 else p_free, 1)
                if not early(g, 2):
                    low_2(g - 2)
                    copy_logits(g - 2)
                    dve.wait_ge(rows_stored[par], 16 * (g - par))
                dve.wait_ge(p_free, g + 1)
                dve.wait_ge(rstd_tok, g + 1)
                for k in range(GT):
                    v_.scalar_tensor_tensor(out=h[:, par, k], in0=u[:, k], scalar=rstd[:, k:k + 1], in1=cb[:, 1],
                                            op0=ALU.mult, op1=ALU.add).then_inc(step, 1)
                for k in range(GT):
                    dve.wait_ge(step, s0 + 5 + k)
                    v_.bn_stats(bst[:, k], h[:, par, k]).then_inc(step, 1)
                for k in range(GT):
                    dve.wait_ge(step, s0 + 7 + k)
                    dve.nop(nofuse=True)
                    v_.bn_aggr(mv[:, k], bst[:, k]).then_inc(step, 1)
                dve.wait_ge(step, s0 + 10)
                v_.tensor_scalar(vln, mv[:, :, 1], EPS_LN, None, ALU.add).then_inc(var_ln, 1)
                dve.wait_ge(rstd_ln, g + 1)
                for k in range(GT):
                    v_.tensor_scalar(xn[:, k], h[:, par, k], mv[:, k, 0:1], rln[:, k:k + 1],
                                     ALU.subtract, ALU.mult).then_inc(xn_ready, 1)
                dve.wait_ge(row_hi, g + 1)
                v_.tensor_tensor(rows[:, par, :, D + D2:2 * D + D2], xn[:], rows[:, par, :, 0:D].bitcast(F32),
                                 ALU.subtract).then_inc(row_lo, 1)

            groups(dve, group)
            low_2(NE - LATE)
            copy_logits(GROUPS - 2)
            low_2(NE - 1)
            copy_logits(GROUPS - 1)
            dve.wait_ge(lg_copied, 1 + GROUPS)

            done = [0]

            def link(ins):
                done[0] += 1
                ins.then_inc(ds, 1)
                dve.wait_ge(ds, done[0])

            def over_e(x):
                return x.unsqueeze(1).to_broadcast((P, TILES, NE))

            def over_t(x):
                return x.unsqueeze(2).to_broadcast((P, TILES, NE))

            src = logits
            for k in range(TOPK):
                ohk = oh[:, k].rearrange("p e t -> p t e")
                link(v_.tensor_reduce(top[:, k], src[:], AX.X, ALU.max))
                link(v_.tensor_tensor(eq[:], src[:], over_t(top[:, k]), ALU.is_equal))
                link(v_.tensor_tensor(eq[:], eq[:], over_e(first_e[:]), ALU.mult))
                link(v_.tensor_reduce(found[:, k], eq[:], AX.X, ALU.max))
                link(v_.tensor_tensor(ohk, over_e(first_e[:]), over_t(found[:, k]), ALU.is_equal))
                if k == 0:
                    link(v_.scalar_tensor_tensor(out=l2[:], in0=ohk, scalar=-BIG, in1=src[:], op0=ALU.mult, op1=ALU.add))
                    src = l2
            v_.tensor_tensor(chosen[:], oh[:, 0], oh[:, 1], ALU.add).then_inc(chosen_ready, 1)
            v_.tensor_tensor(wex[:, 0], top[:, 1], top[:, 0], ALU.subtract).then_inc(top_ready, 1)

            dve.wait_ge(counts_ready, 1)
            link(v_.tensor_copy(tot[:].rearrange("p e t -> p (e t)"), p_disp[:, P:2 * P]))
            link(v_.tensor_tensor_scan(incl[:].rearrange("p e t -> p (e t)"), restart[:].rearrange("p e t -> p (e t)"),
                                       tot[:].rearrange("p e t -> p (e t)"), 0.0, ALU.mult, ALU.add))
            v_.memset(e_one[:], 1.0)
            link(v_.tensor_scalar(e_int[:], incl[:, :, TILES - 1], float(P - 1), None, ALU.add))
            link(v_.tensor_scalar(e_int[:], e_int[:], 7, None, ALU.arith_shift_right))
            link(v_.tensor_copy(e_til[:], e_int[:]))
            link(v_.tensor_tensor_scan(e_end[:], e_one[:], e_til[:], 0.0, ALU.mult, ALU.add))
            link(v_.tensor_tensor(e_til[:], e_end[:], e_til[:], ALU.subtract))
            link(v_.tensor_tensor(incl[:], incl[:], tot[:], ALU.subtract))
            link(v_.scalar_tensor_tensor(out=base[:], in0=e_til[:].unsqueeze(2).to_broadcast((P, NE, TILES)),
                                         scalar=float(P), in1=incl[:], op0=ALU.mult, op1=ALU.add))
            link(v_.tensor_tensor(base[:], base[:], p_disp[:, 0:P].rearrange("p (e t) -> p e t", e=NE), ALU.add))
            for k in range(TOPK):
                link(v_.tensor_tensor(picked[:, k], oh[:, k], base[:], ALU.mult))
            link(v_.tensor_reduce(slot_f[:, 0].rearrange("p (k t) -> p k t", k=TOPK),
                                  picked.rearrange("p k e t -> p k t e"), AX.X, ALU.add))
            link(v_.tensor_copy(slot[:], slot_f[:, 0]))
            link(v_.tensor_scalar(slot_i[:, 0], slot[:], 7, None, ALU.arith_shift_right))
            link(v_.tensor_scalar(slot_i[:, 1], slot[:], P - 1, None, ALU.bitwise_and))
            link(v_.tensor_copy(slot_f[:], slot_i[:]))
            NT = TOPK * TILES
            for k in range(2):
                dve.wait_ge(rows_stored[k], 32 * GROUPS // 2)
            link(v_.tensor_tensor(in_tile[:], tile_no[:, 0:SLOT_TILES].unsqueeze(1).to_broadcast((P, NT, SLOT_TILES)),
                                  slot_f[:, 0].unsqueeze(2).to_broadcast((P, NT, SLOT_TILES)), ALU.is_equal))
            v_.tensor_scalar(part[:, :, 0], in_tile[:], p_plus1[:, 0:1], None, ALU.mult)
            v_.tensor_tensor(part[:, :, 1], in_tile[:], block_no[:].unsqueeze(2).to_broadcast((P, NT, SLOT_TILES)), ALU.mult)
            for q in range(4):
                m = NT // 4
                v_.tensor_tensor(in_row[:, q * m:(q + 1) * m], row128[:].unsqueeze(1).to_broadcast((P, m, P)),
                                 slot_f[:, 1, q * m:(q + 1) * m].unsqueeze(2).to_broadcast((P, m, P)), ALU.is_equal)\
                    .then_inc(hot_ready, 1)
            T1 = SLOT_TILES + 1
            link(v_.tensor_tensor(e_cmp, tile_no[0:1].unsqueeze(2).to_broadcast((1, T1, NE)),
                                  e_end[0:1].unsqueeze(1).to_broadcast((1, T1, NE)), ALU.is_ge))
            link(v_.tensor_reduce(e_sum[:], e_cmp, AX.X, ALU.add))
            v_.tensor_scalar(etab[:], e_sum[:], float(NE - 1), None, ALU.min).then_inc(etab_ready, 1)
            dve.wait_ge(exp_ready, 1)
            link(v_.tensor_scalar(wex[:, 2], wex[:, 1], 1.0, None, ALU.add))
            link(v_.reciprocal(wgt[:, 0], wex[:, 2]))
            v_.tensor_tensor(wgt[:, 1], wex[:, 1], wgt[:, 0], ALU.mult).then_inc(wgt_ready, 1)
            dve.wait_ge(b1_half, 1)
            v_.tensor_tensor(b1_s, b1_s, b1_hi, ALU.subtract).then_inc(b1_placed, 2)
            dve.wait_ge(tab_sums, 1)
            link(v_.tensor_copy(ts[:], p_disp[:, 0:2 * SLOT_TILES].rearrange("p (n a) -> p n a", n=2)))
            link(v_.scalar_tensor_tensor(out=code[:, 0], in0=ts[:, 1], scalar=float(P), in1=ts[:, 0],
                                         op0=ALU.mult, op1=ALU.add))
            link(v_.tensor_scalar(code[:, 1], ts[:, 0], 0.0, None, ALU.is_equal))
            link(v_.tensor_scalar(code_i[:], code[:, 0], -1.0, None, ALU.add))
            v_.tensor_scalar(tab[:, 0, 0:SLOT_TILES], code_i[:], N_TOK - 1, None, ALU.bitwise_and).then_inc(tab_ready, 1)
            link(v_.tensor_tensor(code[:, 2], code[:, 1], pad_row[:], ALU.mult))
            v_.scalar_tensor_tensor(out=tab[:, 1, UNROLL:UNROLL + SLOT_TILES], in0=code[:, 2], scalar=-1.0,
                                    in1=code[:, 0], op0=ALU.add, op1=ALU.add).then_inc(tab_ready, 1)

            def low(j):
                for n, (lo, hi, src_) in enumerate(((0, HA, p_ha[:]), (HA, FF, p_hb[:, 0:FF - HA]))):
                    dve.wait_ge(relu_hi, 2 * j + n + 1)
                    v_.scalar_tensor_tensor(out=h_lo[:, lo:hi], in0=src_, scalar=0.0, in1=h_hi[:, lo:hi].bitcast(F32),
                                            op0=ALU.max, op1=ALU.subtract).then_inc(relu_lo, 1)

            def tile(j, k, more):
                for n, (lo, hi, src_) in enumerate(((0, 4, p_loa), (4, 6, p_lob))):
                    dve.wait_ge(tlo_ready, 2 * j + n + 1)
                    v_.tensor_copy(ht_lo[:, lo:hi], src_[:, 0:(hi - lo) * P].rearrange("p (c t) -> p c t", t=P))\
                        .then_inc(tlo_copied, 1)
                if more:
                    low(j + 1)
                e = dve.value_load(etab[0:1, bass.ds(j, 1)], min_val=0, max_val=NE - 1)
                dve.wait_ge(y_ready, j + 1)
                if not early(j, UNROLL):
                    dve.wait_ge(y_stored[k], (j - k) * 16 // UNROLL)
                v_.tensor_tensor(y_s[:, k], p_y[:, 0:D], b2_s[:, bass.ds(e, 1)].rearrange("p e d -> p (e d)"), ALU.add)\
                    .then_inc(y_copied, 1)

            low(0)
            dve.wait_ge(s_b2, 16)
            for k in range(UNROLL):
                tile(k, k, True)
            with dve.Fori(UNROLL, SLOT_TILES - 2 * UNROLL + 1, UNROLL) as i:
                for k in range(UNROLL):
                    tile(i + k, k, True)
            for k in range(UNROLL):
                tile(SLOT_TILES - UNROLL + k, k, k < 2)
            dve.wait_ge(res_loaded, 16)
            dve.wait_ge(wgt_ready, 1)
            n = TILES // FIN
            for c in range(FIN):
                dve.wait_ge(y_loaded[c], 32)
                for t in range(c * n, (c + 1) * n):
                    v_.scalar_tensor_tensor(out=res_f[:, t], in0=y0_f[:, t], scalar=wgt[:, 0, t:t + 1], in1=res_f[:, t],
                                            op0=ALU.mult, op1=ALU.add).then_inc(mixed, 1)
                for t in range(c * n, (c + 1) * n):
                    dve.wait_ge(mixed, t + 1)
                    ins = v_.scalar_tensor_tensor(out=res_f[:, t], in0=y1_f[:, t], scalar=wgt[:, 1, t:t + 1],
                                                  in1=res_f[:, t], op0=ALU.mult, op1=ALU.add)
                ins.then_inc(out_ready, 1)

        @block.tensor
        def _(pe):
            mm = nc.tensor.matmul
            pe.wait_ge(s_gb, 16)
            for c in range(CORE_CH):
                pe.wait_ge(s_w5[c], 16)
                for s in range(SHIFTS):
                    n = c * SHIFTS + s
                    mm(p_set[0:2, 0:D], gb_s[:, n], w5[:, c, s], start=(n == 0), stop=False)
            pe.wait_ge(s_w5[CORE_CH], 32)
            mm(p_set[0:2, 0:D], gb_s[:, N_W - 2], w5h[:, 0], start=False, stop=False)
            mm(p_set[0:2, 0:D], gb_s[0:HALO_B, N_W - 1], w5h[0:HALO_B, 1], start=False, stop=True).then_inc(row_sums, 1)
            pe.wait_ge(s_small, 16 * 8)
            pe.wait_ge(consts, N_CONST)
            pe.wait_ge(row_copied, 1)
            mm(p_bc[:, 0:D], sel_s[:, 0], cb_row[:], start=True, stop=True)
            mm(p_bc[:, D:2 * D], sel_s[:, 1], cb_row[:], start=True, stop=False)
            mm(p_bc[:, D:2 * D], sel_s[:, 2], bias2_s[:], start=False, stop=False)
            mm(p_bc[:, D:2 * D], attn[:], proj_s[:, 0], start=False, stop=False)
            mm(p_bc[:, D:2 * D], attn[0:D2], proj_s[0:D2, 1], start=False, stop=True).then_inc(bc_ready, 1)
            pe.wait_ge(dset, N_SET)
            pe.wait_ge(hi_r, 1)
            pe.wait_ge(wr_split, 1)

            def squares(t, b, o):
                pe.wait_ge(sq_ready, t + 1)
                for c in range(KCH):
                    r = P if c < KCH - 1 else HALO_B
                    ins = mm(o[:, D + 1:D + 2], xbuf[0:r, b, c], wt[0:r, c, D:D + 1], start=(c == 0), stop=(c == KCH - 1))
                ins.then_inc(sq_used, 1)

            def embed(g, par):
                for k in range(GT):
                    t, b, o = GT * g + k, GT * par + k, p_tok[par][:, k * PC:(k + 1) * PC]
                    pe.wait_ge(x_loaded[b], 16 * (g - par) + 32)
                    if k == 0 and not early(g, 2):
                        pe.wait_ge(p_free, g - 1)
                    for c in range(KCH):
                        r = P if c < KCH - 1 else HALO_B
                        ins = mm(o[:, 0:D + 1], xbuf[0:r, b, c], wt[0:r, c, 0:D + 1], start=(c == 0), stop=(c == KCH - 1))
                    ins.then_inc(x_used, 1)
                    if k == 1:
                        squares(t - 1, b - 1, p_tok[par][:, 0:PC])
                    elif not early(g, 1):
                        squares(t - 1, (b - 1) % 4, p_tok[1 - par][:, PC:2 * PC])
                    if k == 0 and not early(g, 2):
                        turn_rows(g - 2, par)

            def split_product(o, x, a, b, c, d, e):
                mm(o, x[:, 0:P], a, start=True, stop=False)
                mm(o, x[:, 0:P], b, start=False, stop=False)
                mm(o, x[:, 2 * P:3 * P], c, start=False, stop=False)
                mm(o, x[:, P:2 * P], d, start=False, stop=False)
                return mm(o, x[0:e.shape[0], 3 * P:4 * P], e, start=False, stop=True)

            def route(g):
                for k in range(GT):
                    pe.wait_ge(xts_ready, GT * g + k + 1)
                    if k == 0:
                        pe.wait_ge(lg_copied, g + 1)
                    ins = split_product(p_lg[:, k * NE:(k + 1) * NE], xts[k], wr_hi[:], wr_lo[:], wr_hi[:], wr_2[:],
                                        wr_2[0:D2])
                ins.then_inc(lg_ready, 1)

            def turn(o, x):
                for q in range(ROW // P):
                    ins = nc.tensor.transpose(o[:, q * P:(q + 1) * P].bitcast(F32R), x[:, q * P:(q + 1) * P], identr[:])
                return ins

            def turn_rows(g, par):
                pe.wait_ge(row_lo, g + 1)
                for k in range(GT):
                    turn(p_xt[k], rows[:, par, k]).then_inc(xt_ready, 1)

            def group(g, par):
                embed(g, par)
                if not early(g, 2):
                    route(g - 2)

            groups(pe, group)
            squares(TILES - 1, 3, p_tok[1][:, PC:2 * PC])
            turn_rows(GROUPS - 2, 0)
            route(GROUPS - 2)
            turn_rows(GROUPS - 1, 1)
            route(GROUPS - 1)

            pe.wait_ge(chosen_ready, 1)
            ch = chosen[:].rearrange("p e t -> p (e t)")
            mm(p_disp[:, 0:P], tri[:], ch, start=True, stop=True)
            mm(p_disp[:, P:2 * P], onesb[:], ch, start=True, stop=True).then_inc(counts_ready, 1)
            NT = TOPK * TILES
            for n in range(NT):
                if n % (NT // 4) == 0:
                    pe.wait_ge(hot_ready, n // (NT // 4) + 1)
                ins = mm(p_disp[:, 0:2 * SLOT_TILES], in_row[:, n], part[:, n].rearrange("p a b -> p (a b)"),
                         start=(n == 0), stop=(n == NT - 1))
            ins.then_inc(tab_sums, 1)

            def gathered(j, k):
                pe.wait_ge(g_loaded[k], 16 * (j - k) // UNROLL + 16)
                turn(p_x, gath[:, k]).then_inc(gx_ready, 1)

            def first_product(j, k):
                e = pe.value_load(etab[0:1, bass.ds(j, 1)], min_val=0, max_val=NE - 1)
                pe.wait_ge(gxs_ready, j + 1)
                for o, lo, hi, s in ((p_ha, 0, HA, ha_ready), (p_hb, HA, FF, hb_ready)):
                    a, b, c, d = (w[:, bass.ds(e, 1), lo:hi].rearrange("p e f -> p (e f)") for w in (w1_hi, w1_lo, w1_2, w1_b[0:D2 + 2]))
                    ins = split_product(o[:, 0:hi - lo], xts[k], a, b, a, c, d)
                    ins.then_inc(s, 1)
                return ins

            def turn_hidden(j):
                for n, (o, lo, hi) in enumerate(((p_hia, 0, 4), (p_hib, 4, 6))):
                    pe.wait_ge(relu_hi, 2 * j + n + 1)
                    for c in range(lo, hi):
                        ins = nc.tensor.transpose(o[:, (c - lo) * P:(c - lo + 1) * P].bitcast(F32R), h_hi[:, c * P:(c + 1) * P],
                                                  identr[:])
                    ins.then_inc(thi_ready, 1)
                for n, (o, lo, hi) in enumerate(((p_loa, 0, 4), (p_lob, 4, 6))):
                    pe.wait_ge(relu_lo, 2 * j + n + 1)
                    for c in range(lo, hi):
                        ins = nc.tensor.transpose(o[:, (c - lo) * P:(c - lo + 1) * P].bitcast(F32R), h_lo[:, c * P:(c + 1) * P],
                                                  identr[:])
                    ins.then_inc(tlo_ready, 1)

            def second_product(j):
                e = pe.value_load(etab[0:1, bass.ds(j, 1)], min_val=0, max_val=NE - 1)
                w = [[w2s[:, bass.ds(e, 1), n, c].rearrange("p e d -> p (e d)") for c in range(FCH)] for n in range(2)]
                pe.wait_ge(thi_copied, 2 * j + 2)
                if not early(j, 1):
                    pe.wait_ge(y_copied, j)
                for c in range(FCH):
                    mm(p_y[:, 0:D], ht_hi[:, c], w[0][c], start=(c == 0), stop=False)
                    mm(p_y[:, 0:D], ht_hi[:, c], w[1][c], start=False, stop=False)
                pe.wait_ge(tlo_copied, 2 * j + 2)
                for c in range(FCH):
                    ins = mm(p_y[:, 0:D], ht_lo[:, c], w[0][c], start=False, stop=(c == FCH - 1))
                ins.then_inc(y_ready, 1)

            def tile(j, k, more, more2):
                if more:
                    ins = first_product(j + 1, (k + 1) % UNROLL)
                second_product(j)
                if more2:
                    gathered_next(j, k)
                if more:
                    turn_hidden(j + 1)

            def gathered_next(j, k):
                k2 = (k + 2) % UNROLL
                pe.wait_ge(g_loaded[k2], 16 * ((j - k) // UNROLL + (k + 2) // UNROLL) + 16)
                turn(p_x, gath[:, k2]).then_inc(gx_ready, 1)

            pe.wait_ge(etab_ready, 1)
            for k in range(2):
                pe.wait_ge(g_loaded[k], 16)
                if k:
                    pe.wait_ge(gxs_ready, 1)
                turn(p_x, gath[:, k]).then_inc(gx_ready, 1)
            pe.wait_ge(lo_a, NE)
            pe.wait_ge(lo_b, NE)
            pe.wait_ge(lo_2, NE + 1)
            pe.wait_ge(b1_placed, 34)
            first_product(0, 0)
            turn_hidden(0)
            with pe.Fori(0, SLOT_TILES - 2 * UNROLL + 1, UNROLL) as i:
                for k in range(UNROLL):
                    tile(i + k, k, True, True)
            j = SLOT_TILES - UNROLL
            tile(j, 0, True, True)
            tile(j + 1, 1, True, False)
            tile(j + 2, 2, False, False)


def kernel(x, L0_tok_gamma, L0_tok_beta, L0_tok_W, L0_tok_b, L0_attn_proj_w, L0_attn_proj_b, L0_ffn_Wr, L0_ffn_W1,
           L0_ffn_b1, L0_ffn_W2, L0_ffn_b2):
    import concourse.bacc as bacc
    from concourse.bass_utils import run_bass_kernel_spmd

    x = np.asarray(x)
    patches = x.reshape(IMAGES, GRID, PATCH, GRID, PATCH, CH).transpose(0, 1, 3, 2, 4, 5)
    pad = np.zeros((IMAGES, SIDE + 2, SIDE + 2, CH), x.dtype)
    pad[:, 1:-1, 1:-1] = x
    lo, hi = slice(0, SIDE, PATCH), slice(PATCH + 1, SIDE + 2, PATCH)

    def across(a):
        return a.reshape(IMAGES, GRID, PATCH, GRID, CH).transpose(0, 1, 3, 2, 4).reshape(N_TOK, -1)

    def along(a):
        return a.reshape(IMAGES, GRID, GRID, PATCH, CH).reshape(N_TOK, -1)

    halo = np.concatenate([across(pad[:, 1:-1, lo]), across(pad[:, 1:-1, hi]),
                           along(pad[:, lo, 1:-1]), along(pad[:, hi, 1:-1])], axis=1)
    pix = np.concatenate([patches.reshape(N_TOK, CORE), halo], axis=1)
    pix = pix.reshape(TILES, P, CORE + HALO).transpose(0, 2, 1)
    full = (KCH - 1) * P
    pix_a = pix[:, :full].reshape(TILES, KCH - 1, P, P).transpose(0, 2, 1, 3)
    w_core, w_halo = by_slab(np.asarray(L0_tok_W))
    gb = np.stack([np.asarray(L0_tok_gamma), np.asarray(L0_tok_beta)], axis=1)
    g_core, g_halo = by_slab(gb)
    gb_s = np.zeros((P, N_W, 2), gb.dtype)
    gb_s[:, :CORE_CH * SHIFTS] = g_core.transpose(1, 0, 2, 3).reshape(P, -1, 2)
    gb_s[:, -2] = g_halo[:P]
    gb_s[:HALO_B, -1] = g_halo[P:]
    sel = np.zeros((2, 3, P), np.float32)
    sel[0, 0], sel[1, 1], sel[:, 2] = 1, 1, 1
    arrays = {
        "pix_a": pix_a, "pix_b": pix[:, full:], "w_core": w_core, "w_halo": w_halo, "gb": gb_s,
        "count": feature_maps()[2], "sel": sel,
        "bias2": np.stack([np.asarray(L0_tok_b), np.asarray(L0_attn_proj_b)]),
        "proj_t": np.asarray(L0_attn_proj_w).T, "wr": L0_ffn_Wr, "w1": L0_ffn_W1, "b1": L0_ffn_b1,
        "w2": L0_ffn_W2, "b2": L0_ffn_b2,
    }
    arrays = {n: np.ascontiguousarray(a) for n, a in arrays.items()}
    nc = bacc.Bacc("TRN2", target_bir_lowering=False, num_devices=1)
    args = [nc.dram_tensor(n, a.shape, mybir.dt.from_np(a.dtype), kind="ExternalInput").ap()
            for n, a in arrays.items()]
    args.append(nc.dram_tensor("out", (N_TOK, D), F32, kind="ExternalOutput").ap())
    vit_tower_kernel(nc, *args)
    r = run_bass_kernel_spmd(nc, [arrays], core_ids=[0])
    return r.results[0]["out"].reshape(IMAGES, GRID * GRID, D)
```

```python
from contextlib import ExitStack

import numpy as np
import concourse.bass as bass
from concourse import mybir

ALU = mybir.AluOpType
ACT = mybir.ActivationFunctionType
AX = mybir.AxisListType
F32 = mybir.dt.float32
F32R = mybir.dt.float32r
BF16 = mybir.dt.bfloat16
I32 = mybir.dt.int32
U32 = mybir.dt.uint32

P = 128
IMAGES, SIDE, CH = 32, 128, 3
PATCH = 16
GRID = SIDE // PATCH
SHIFTS = 5
D = 192
N_TOK = IMAGES * GRID * GRID
FEAT = PATCH * PATCH * SHIFTS * CH
CORE = PATCH * PATCH * CH
HALO = 4 * PATCH * CH
CORE_CH = CORE // P
KCH = CORE_CH + 2
HALO_B = HALO - P
N_W = CORE_CH * SHIFTS + 2
TILES = N_TOK // P
GT = 2
GROUPS = TILES // GT
EPS_TOK, EPS_LN = 1e-3, 1e-5
NE, TOPK = 8, 2
FF = 4 * D
FCH = FF // P
HA = 512
D2 = D - P
ROW = 2 * D
TAIL = ROW - D2
ROW_P = ROW + D2
SLOT_TILES = TOPK * N_TOK // P + NE - 1
UNROLL = 3
assert SLOT_TILES % UNROLL == 0
LATE = 2
PC = 256
BIG = 3e38


def core_order():
    edge = np.zeros((PATCH, PATCH, CH), int)
    edge[[0, -1]] += 1
    edge[:, [0, -1]] += 1
    kinds = [np.flatnonzero(edge.ravel() == n).reshape(-1, CORE_CH) for n in range(3)]
    return np.concatenate(kinds).T.ravel()


def feature_maps():
    def feat(i, j, s, c):
        return (i * PATCH + j) * SHIFTS * CH + s * CH + c

    core = np.full((CORE, SHIFTS), FEAT)
    for i in range(PATCH):
        for j in range(PATCH):
            shown = ((i, j), (i, j + 1), (i, j - 1), (i + 1, j), (i - 1, j))
            for s, (a, b) in enumerate(shown):
                if 0 <= a < PATCH and 0 <= b < PATCH:
                    for c in range(CH):
                        core[(i * PATCH + j) * CH + c, s] = feat(a, b, s, c)
    core = core[core_order()]
    last = PATCH - 1
    sides = [[feat(i, 0, 1, c) for i in range(PATCH) for c in range(CH)],
             [feat(i, last, 2, c) for i in range(PATCH) for c in range(CH)],
             [feat(0, j, 3, c) for j in range(PATCH) for c in range(CH)],
             [feat(last, j, 4, c) for j in range(PATCH) for c in range(CH)]]
    halo = np.concatenate(sides)
    count = np.concatenate([(core < FEAT).sum(1), np.ones(HALO), np.zeros(P - HALO_B)])
    return core, halo, count.reshape(KCH, P).T.astype(np.float32)


def by_slab(w):
    core, halo, _ = feature_maps()
    padded = np.concatenate([w, np.zeros((1, w.shape[1]), w.dtype)])
    return padded[core].reshape(CORE_CH, P, SHIFTS, -1), w[halo]



def vit_tower_kernel(nc, pix_a, pix_b, w_core, w_halo, gb, count, sel, bias2, proj_t, wr, w1, b1, w2,
                     b2, out):
    ctx = ExitStack()
    with ctx:
        def sem(name):
            return ctx.enter_context(nc.semaphore(name))

        def sb(name, shape, dt=F32, stack=ctx):
            return stack.enter_context(nc.sbuf_tensor(name, shape, dt))

        xrow_d = nc.dram_tensor("xrow_d", [N_TOK, ROW], F32)
        resid_d = nc.dram_tensor("resid_d", [N_TOK, D], F32)
        y_d = nc.dram_tensor("y_d", [TOPK * N_TOK + SLOT_TILES * P, D], F32)

        fin = ExitStack()
        res_f = sb("res_f", [P, TILES, D], stack=fin)
        y0_f = sb("y0_f", [P, TILES, D], stack=fin)
        y1_f = sb("y1_f", [P, TILES, D], stack=fin)
        fin.close()
        w1_hi = sb("w1_hi", [P, NE, FF], F32R)
        w1_lo = sb("w1_lo", [P, NE, FF], F32R)
        w1_2 = sb("w1_2", [P, NE, FF], F32R)
        setup = ExitStack()
        w5 = sb("w5", [P, CORE_CH, SHIFTS, D], stack=setup)
        w5h = sb("w5h", [P, 2, D], stack=setup)
        setup.close()
        w1_b = sb("w1_b", [P, NE, FF], F32R)
        pixels = ExitStack()
        sb("w2s_first", [P, NE - LATE, FCH, 2, D], F32R, stack=pixels)
        xbuf = sb("xbuf", [P, 4, KCH, P], stack=pixels)
        attn = sb("attn", [P, P], stack=pixels)
        proj_s = sb("proj_s", [P, 2, D], stack=pixels)
        pixels.close()
        w2s = sb("w2s", [P, NE, FCH, 2, D], F32R)

        identr = sb("identr", [P, P], F32R)
        xts = [sb(f"xts{k}", [P, 4 * P], F32R)[:] for k in range(GT)]
        logits = sb("logits", [P, TILES, NE])
        wgt = sb("wgt", [P, TOPK, TILES])
        tab = sb("tab", [P, 2, SLOT_TILES + UNROLL], I32)
        etab = sb("etab", [1, SLOT_TILES + 1], I32)
        tri = sb("tri", [P, P], BF16)
        onesb = sb("onesb", [P, P], BF16)
        row128 = sb("row128", [P, P], BF16)
        tile_no = sb("tile_no", [P, SLOT_TILES + 1])
        pad_row = sb("pad_row", [P, SLOT_TILES])
        first_e = sb("first_e", [P, NE])
        block_no = sb("block_no", [P, TOPK * TILES])
        p_plus1 = sb("p_plus1", [P, 1])
        restart = sb("restart", [P, NE, TILES])
        raws = ExitStack()
        raw_a = sb("raw_a", [P, FF], stack=raws)
        raw_b = sb("raw_b", [P, FF], stack=raws)
        raw_2 = sb("raw_2", [P, FCH, D], stack=raws)
        raws.close()
        h_hi = sb("h_hi", [P, FF], F32R)
        h_lo = sb("h_lo", [P, FF], F32R)
        ht_hi = sb("ht_hi", [P, FCH, P], F32R)
        sb("rest_of_raw_2", [P, FCH * D - FF])

        emb = ExitStack()
        wt = sb("wt", [P, KCH, D + 2], stack=emb)
        gb_s = sb("gb_s", [P, N_W, 2], stack=emb)
        cnt_s = sb("cnt_s", [P, KCH], stack=emb)
        cb = sb("cb", [P, 2, D], stack=emb)
        rows = sb("rows", [P, 2, GT, ROW_P], F32R, stack=emb)
        first = ExitStack()
        sel_s = sb("sel_s", [2, 3, P], stack=first)
        bias2_s = sb("bias2_s", [2, D], stack=first)
        cb_row = sb("cb_row", [2, D], stack=first)
        ident = sb("ident", [P, P], stack=first)
        ints = sb("ints", [P, P], I32, stack=first)
        first.close()
        h = sb("h", [P, 2, GT, D], stack=emb)
        xn = sb("xn", [P, GT, D], stack=emb)
        u = xn
        small = sb("small", [P, 8, GT], stack=emb)
        bst = sb("bst", [P, GT, 6], stack=emb)
        mv = sb("mv", [P, GT, 2], stack=emb)
        minus_half = sb("minus_half", [P, GT], stack=emb)
        wr_raw = sb("wr_raw", [P, 2, NE], stack=emb)
        wr_hi = sb("wr_hi", [P, NE], F32R, stack=emb)
        wr_lo = sb("wr_lo", [P, NE], F32R, stack=emb)
        wr_2 = sb("wr_2", [P, NE], F32R, stack=emb)
        wr_b = sb("wr_b", [D2, NE], F32R, stack=emb)
        emb.close()

        disp = ExitStack()
        oh = sb("oh", [P, TOPK, NE, TILES], stack=disp)
        eq = sb("eq", [P, TILES, NE], stack=disp)
        l2 = sb("l2", [P, TILES, NE], stack=disp)
        top = sb("top", [P, TOPK, TILES], stack=disp)
        found = sb("found", [P, TOPK, TILES], stack=disp)
        chosen = sb("chosen", [P, NE, TILES], BF16, stack=disp)
        tot = sb("tot", [P, NE, TILES], stack=disp)
        incl = sb("incl", [P, NE, TILES], stack=disp)
        base = sb("base", [P, NE, TILES], stack=disp)
        spare = raw_2[:].rearrange("p c d -> p (c d)")
        picked = spare[:, 0:TOPK * NE * TILES].rearrange("p (k e t) -> p k e t", k=TOPK, e=NE)
        after = TOPK * NE * TILES
        e_cmp = spare[0:1, after:after + (SLOT_TILES + 1) * NE].rearrange("p (a e) -> p a e", e=NE)
        e_int = sb("e_int", [P, NE], I32, stack=disp)
        e_til = sb("e_til", [P, NE], stack=disp)
        e_end = sb("e_end", [P, NE], stack=disp)
        e_one = sb("e_one", [P, NE], stack=disp)
        slot = sb("slot", [P, TOPK * TILES], I32, stack=disp)
        slot_i = sb("slot_i", [P, 2, TOPK * TILES], I32, stack=disp)
        slot_f = sb("slot_f", [P, 2, TOPK * TILES], stack=disp)
        part = sb("part", [P, TOPK * TILES, 2, SLOT_TILES], BF16, stack=disp)
        in_tile = sb("in_tile", [P, TOPK * TILES, SLOT_TILES], BF16, stack=disp)
        in_row = sb("in_row", [P, TOPK * TILES, P], BF16, stack=disp)
        ts = sb("ts", [P, 2, SLOT_TILES], stack=disp)
        code = sb("code", [P, 3, SLOT_TILES], stack=disp)
        code_i = sb("code_i", [P, SLOT_TILES], I32, stack=disp)
        e_sum = sb("e_sum", [1, SLOT_TILES + 1], stack=disp)
        wex = sb("wex", [P, 3, TILES], stack=disp)
        disp.close()

        b1_s, b1_hi = raw_a[0:NE], raw_b[0:NE]

        xts.append(sb("xts2", [P, 4 * P], F32R)[:])
        b2_s = sb("b2_s", [P, NE, D])
        gath = sb("gath", [P, UNROLL, ROW_P], F32R)
        ht_lo = sb("ht_lo", [P, FCH, P], F32R)
        y_s = sb("y_s", [P, UNROLL, D])
        idx = sb("idx", [P, 2, 2, UNROLL], U32)

        bank = [ctx.enter_context(nc.psum_tensor(f"bank{n}", [P, 512], F32)) for n in range(8)]
        p_tok = bank[0:2]
        p_xt = [bank[2], bank[3]]
        p_lg, p_set, p_bc, p_disp = bank[4], bank[5], bank[6], bank[7]
        p_ha, p_hb, p_hia, p_hib, p_loa, p_lob, p_y, p_x = bank

        s_gb, s_small, s_b2, s_b1 = sem("s_gb"), sem("s_small"), sem("s_b2"), sem("s_b1")
        s_w5 = [sem(f"s_w5_{c}") for c in range(CORE_CH + 1)]
        x_loaded = [sem(f"x_loaded{b}") for b in range(4)]
        raw_a_loaded, raw_b_loaded, raw_2_loaded = sem("raw_a_loaded"), sem("raw_b_loaded"), sem("raw_2_loaded")
        consts = sem("consts")
        row_sums = sem("row_sums")
        row_copied = sem("row_copied")
        bc_ready = sem("bc_ready")
        scaled = sem("scaled")
        dset = sem("dset")
        x_used = sem("x_used")
        sq_ready = sem("sq_ready")
        sq_folded = sem("sq_folded")
        sq_used = sem("sq_used")
        p_free = sem("p_free")
        step = sem("step")
        var_tok, rstd_tok = sem("var_tok"), sem("rstd_tok")
        var_ln, rstd_ln = sem("var_ln"), sem("rstd_ln")
        xn_ready, row_hi, row_lo = sem("xn_ready"), sem("row_hi"), sem("row_lo")
        xt_ready, xts_ready = sem("xt_ready"), sem("xts_ready")
        lg_ready, lg_copied = sem("lg_ready"), sem("lg_copied")
        rows_stored = [sem(f"rows_stored{k}") for k in range(2)]
        hi_a, hi_b, lo_a, lo_b = sem("hi_a"), sem("hi_b"), sem("lo_a"), sem("lo_b")
        hi_2, lo_2 = sem("hi_2"), sem("lo_2")
        ds = sem("ds")
        chosen_ready, counts_ready = sem("chosen_ready"), sem("counts_ready")
        top_ready, exp_ready = sem("top_ready"), sem("exp_ready")
        tile_ready, part_ready = sem("tile_ready"), sem("part_ready")
        hot_ready, tab_sums = sem("hot_ready"), sem("tab_sums")
        tab_ready, etab_ready = sem("tab_ready"), sem("etab_ready")
        b1_placed = sem("b1_placed")
        g_loaded = [sem(f"g_loaded{k}") for k in range(UNROLL)]
        idx_staged, ones_ready = sem("idx_staged"), sem("ones_ready")
        gx_ready, gxs_ready = sem("gx_ready"), sem("gxs_ready")
        ha_ready, hb_ready = sem("ha_ready"), sem("hb_ready")
        relu_hi, relu_lo = sem("relu_hi"), sem("relu_lo")
        thi_ready, tlo_ready = sem("thi_ready"), sem("tlo_ready")
        thi_copied, tlo_copied = sem("thi_copied"), sem("tlo_copied")
        y_ready, y_half, y_copied = sem("y_ready"), sem("y_half"), sem("y_copied")
        y_stored = [sem(f"y_stored{k}") for k in range(UNROLL)]
        res_loaded = sem("res_loaded")
        FIN = 4
        y_loaded = [sem(f"y_loaded{c}") for c in range(FIN)]
        mixed, out_ready, stored = sem("mixed"), sem("out_ready"), sem("stored")
        int_made, hi_r, wr_split, cb_ready = sem("int_made"), sem("hi_r"), sem("wr_split"), sem("cb_ready")
        b1_half, wgt_ready = sem("b1_half"), sem("wgt_ready")
        N_CONST = 12
        ALL_STORED = 1 + 32 * GROUPS // 2
        N_SET = (SHIFTS - 1) * CORE_CH + 3
        STEPS = 10

        block = ctx.enter_context(nc.Block())

        def early(g, n):
            return isinstance(g, int) and g < n

        def groups(eng, group):
            for g in range(2):
                group(g, g)
            with eng.Fori(2, GROUPS - 1, 2) as i:
                for par in range(2):
                    group(i + par, par)

        @block.sync
        def _(sp):
            sp.dma_start(gb_s[:], gb).then_inc(s_gb, 16)
            for c in range(CORE_CH):
                sp.dma_start(w5[:, c], w_core[c]).then_inc(s_w5[c], 16)
            sp.dma_start(w5h[:, 0], w_halo[0:P]).then_inc(s_w5[CORE_CH], 16)
            sp.dma_start(w5h[0:HALO_B, 1], w_halo[P:HALO]).then_inc(s_w5[CORE_CH], 16)
            sp.dma_start(cnt_s[:], count).then_inc(s_small, 16)
            sp.dma_start(sel_s[:], sel).then_inc(s_small, 16)
            sp.dma_start(bias2_s[:], bias2).then_inc(s_small, 16)
            sp.dma_start(proj_s[:, 0], proj_t[0:P]).then_inc(s_small, 16)
            sp.dma_start(proj_s[0:D2, 1], proj_t[P:D]).then_inc(s_small, 16)
            sp.dma_start(wr_raw[:, 0], wr[0:P]).then_inc(s_small, 16)
            sp.dma_start(wr_raw[0:D2, 1], wr[P:D]).then_inc(s_small, 16)
            sp.dma_start(wr_raw[D2:P, 1], wr[P:D]).then_inc(s_small, 16)

            def group(g, par):
                for k in range(GT):
                    t, b = GT * g + k, GT * par + k
                    if not early(g, 2):
                        sp.wait_ge(sq_used, t - 3)
                    sp.dma_start(xbuf[:, b, 0:KCH - 1], pix_a[bass.ds(t, 1)].rearrange("o p k t -> p (o k) t"))\
                        .then_inc(x_loaded[b], 16)
                    sp.dma_start(xbuf[0:HALO_B, b, KCH - 1], pix_b[bass.ds(t, 1)].rearrange("o p t -> p (o t)"))\
                        .then_inc(x_loaded[b], 16)
                if not early(g, 1):
                    sp.wait_ge(lo_a, g)
                sp.dma_start(raw_a[:], w1[bass.ds(g, 1), 0:P].rearrange("e p f -> p (e f)")).then_inc(raw_a_loaded, 16)
                if not early(g, 1):
                    sp.wait_ge(lo_b, g)
                for lo in (0, D2):
                    sp.dma_start(raw_b[lo:lo + D2], w1[bass.ds(g, 1), P:D].rearrange("e p f -> p (e f)"))\
                        .then_inc(raw_b_loaded, 16)
                if not early(g, 2):
                    sp.wait_ge(lo_2, g - 1)
                    sp.dma_start(raw_2[:], w2[bass.ds(g - 2, 1)].rearrange("e (c p) d -> p (e c) d", p=P))\
                        .then_inc(raw_2_loaded, 16)

            groups(sp, group)
            for e in range(NE - LATE, NE):
                sp.wait_ge(lo_2, e + 1)
                sp.dma_start(raw_2[:], w2[e].rearrange("(c p) d -> p c d", p=P)).then_inc(raw_2_loaded, 16)
                if e == NE - LATE:
                    sp.wait_ge(lo_a, NE)
                    sp.wait_ge(lo_b, NE)
                    sp.dma_start(b1_s, b1).then_inc(s_b1, 16)
            sp.wait_ge(b1_placed, 2)
            sp.dma_start(w1_b[D2:D2 + 1].bitcast(F32), b1_hi).then_inc(b1_placed, 16)
            sp.dma_start(w1_b[D2 + 1:D2 + 2].bitcast(F32), b1_s).then_inc(b1_placed, 16)
            sp.wait_ge(tab_ready, 2)
            sp.wait_ge(etab_ready, 1)
            sp.wait_ge(b1_placed, 34)
            sp.dma_start(b2_s[:].rearrange("p e d -> p (e d)"),
                         b2.rearrange("(o e) d -> o (e d)", o=1).to_broadcast((P, NE * D))).then_inc(s_b2, 16)
            sp.wait_ge(hb_ready, SLOT_TILES)
            for k in range(2):
                sp.wait_ge(rows_stored[k], ALL_STORED)
            sp.dma_start(res_f[:], resid_d[:].rearrange("(t p) d -> p t d", p=P)).then_inc(res_loaded, 16)
            for k in range(UNROLL):
                sp.wait_ge(y_stored[k], 16 * (SLOT_TILES // UNROLL))
            n = TILES // FIN
            for c in range(FIN):
                for k, buf in enumerate((y0_f, y1_f)):
                    at = k * N_TOK + c * n * P
                    sp.dma_start(buf[:, c * n:(c + 1) * n],
                                 y_d[at:at + n * P].rearrange("(t p) d -> p t d", p=P)).then_inc(y_loaded[c], 16)
            for c in range(FIN):
                sp.wait_ge(out_ready, c + 1)
                sp.dma_start(out[c * n * P:(c + 1) * n * P].rearrange("(t p) d -> p t d", p=P),
                             res_f[:, c * n:(c + 1) * n]).then_inc(stored, 16)
            sp.wait_ge(stored, 16 * FIN)

        @block.gpsimd
        def _(pool):
            g_ = nc.gpsimd
            g_.memset(ident[:], 1.0).then_inc(consts, 1)
            g_.memset(tri[:], 1.0).then_inc(consts, 1)
            g_.memset(onesb[:], 1.0).then_inc(consts, 1)
            g_.memset(minus_half[:], -0.5).then_inc(consts, 1)
            g_.memset(rows[:].bitcast(F32), 0.0).then_inc(consts, 1)
            g_.memset(restart[:], 1.0).then_inc(consts, 1)
            pool.wait_ge(consts, 6)
            g_.affine_select(out=ident[:], in_=ident[:], compare_op=ALU.is_equal, fill=0.0, base=0,
                             pattern=[[-1, P]], channel_multiplier=1).then_inc(consts, 1)
            g_.affine_select(out=tri[:], in_=tri[:], compare_op=ALU.is_gt, fill=0.0, base=0,
                             pattern=[[1, P]], channel_multiplier=-1).then_inc(consts, 1)
            g_.memset(rows[:, :, :, ROW:ROW + 2].bitcast(F32), 1.0).then_inc(consts, 1)
            g_.memset(restart[:, :, 0:1], 0.0).then_inc(consts, 1)

            def floats(out_, n, pattern, base_, cm):
                g_.iota(ints[:, 0:n], pattern=pattern, base=base_, channel_multiplier=cm).then_inc(int_made, 1)
                made[0] += 1
                pool.wait_ge(int_made, made[0])
                g_.tensor_copy(out_, ints[:, 0:n]).then_inc(int_made, 1)
                made[0] += 1
                pool.wait_ge(int_made, made[0])

            made = [0]
            floats(first_e[:], NE, [[-1, NE]], NE, 0)
            floats(row128[:], P, [[1, P]], 0, 0)
            floats(tile_no[:], SLOT_TILES + 1, [[1, SLOT_TILES + 1]], 0, 0)
            floats(pad_row[:], SLOT_TILES, [[P, SLOT_TILES]], TOPK * N_TOK + 1, 1)
            floats(block_no[:], TOPK * TILES, [[1, TOPK * TILES]], 0, 0)
            floats(p_plus1[:], 1, [[0, 1]], 1, 1)
            g_.memset(attn[:], 0.0).then_inc(consts, 1)
            g_.memset(tab[:, 1, 0:UNROLL], 0).then_inc(consts, 1)

            def rsqrt(to, frm, signal):
                g_.tensor_tensor(small[:, to], small[:, frm], minus_half[:], ALU.pow).then_inc(signal, 1)

            def flat(w, e):
                return w[:, bass.ds(e, 1)].rearrange("p e f -> p (e f)")

            def group(g, par):
                if not early(g, 2):
                    pool.wait_ge(rstd_ln, g - 1)
                pool.wait_ge(hi_a, g + 1)
                pool.nop(nofuse=True)
                g_.tensor_tensor(flat(w1_lo, g), raw_a[:], flat(w1_hi, g).bitcast(F32), ALU.subtract).then_inc(lo_a, 1)
                pool.wait_ge(lo_a, g + 1)
                if not early(g, 1):
                    pool.wait_ge(var_tok, g)
                    rsqrt(4, 3, rstd_tok)
                    pool.wait_ge(rstd_tok, g)
                pool.wait_ge(hi_b, g + 1)
                pool.nop(nofuse=True)
                g_.tensor_tensor(flat(w1_b[0:D2], g), raw_b[0:D2], flat(w1_2[0:D2], g).bitcast(F32),
                                 ALU.subtract).then_inc(lo_b, 1)
                pool.wait_ge(lo_b, g + 1)
                if not early(g, 1):
                    pool.wait_ge(var_ln, g)
                    rsqrt(6, 5, rstd_ln)

            pool.wait_ge(consts, N_CONST)
            groups(pool, group)
            pool.wait_ge(rstd_ln, GROUPS - 1)
            pool.wait_ge(var_tok, GROUPS)
            rsqrt(4, 3, rstd_tok)
            pool.wait_ge(rstd_tok, GROUPS)
            pool.wait_ge(var_ln, GROUPS)
            rsqrt(6, 5, rstd_ln)

            NT = TOPK * TILES
            pool.wait_ge(rstd_ln, GROUPS)
            pool.wait_ge(tile_ready, 1)
            g_.tensor_tensor(part[:, :, 1], in_tile[:], block_no[:].unsqueeze(2).to_broadcast((P, NT, SLOT_TILES)),
                             ALU.mult).then_inc(part_ready, 1)

            def gather(k, ix):
                g_.indirect_dma_start(out=gath[:, k, 0:ROW].bitcast(F32), out_offset=None, in_=xrow_d[:],
                                      in_offset=bass.IndirectOffsetOnAxis(ap=ix, axis=0)).then_inc(g_loaded[k], 16)

            def scatter(k, ix):
                g_.indirect_dma_start(out=y_d[:], out_offset=bass.IndirectOffsetOnAxis(ap=ix, axis=0),
                                      in_=y_s[:, k], in_offset=None).then_inc(y_stored[k], 16)

            pool.wait_ge(tab_ready, 2)
            pool.wait_ge(etab_ready, 1)
            pool.wait_ge(b1_placed, 34)
            for k in range(2):
                pool.wait_ge(rows_stored[k], ALL_STORED)
            g_.memset(gath[:, :, ROW:ROW + 2].bitcast(F32), 1.0).then_inc(ones_ready, 1)
            g_.memset(gath[:, :, ROW + 2:ROW_P].bitcast(F32), 0.0).then_inc(ones_ready, 1)
            for k in range(UNROLL):
                gather(k, tab[:, 0, k:k + 1].bitcast(U32))

            def turn(j, par):
                g_.tensor_copy(idx[:, par].bitcast(I32), tab[:, :, bass.ds(j + UNROLL, UNROLL)]).then_inc(idx_staged, 1)
                for k in range(UNROLL):
                    pool.wait_ge(gx_ready, j + k + 1)
                    if k == 0:
                        pool.wait_ge(idx_staged, (j + UNROLL) // UNROLL if isinstance(j, int) else j // UNROLL + 1)
                    pool.nop(nofuse=True)
                    gather(k, idx[:, par, 0, k:k + 1])
                    pool.wait_ge(y_copied, j + k + 1)
                    pool.nop(nofuse=True)
                    scatter(k, idx[:, par, 1, k:k + 1])

            with pool.Fori(0, SLOT_TILES - 3 * UNROLL + 1, 2 * UNROLL) as i:
                for par in range(2):
                    turn(i + par * UNROLL, par)
            for k in range(UNROLL):
                j = SLOT_TILES - UNROLL + k
                pool.wait_ge(y_copied, j + 1)
                scatter(k, tab[:, 1, j + UNROLL:j + UNROLL + 1].bitcast(U32))

        @block.scalar
        def _(act):
            a_ = nc.scalar
            act.wait_ge(s_gb, 16)
            for c in range(CORE_CH):
                act.wait_ge(s_w5[c], 16)
                a_.activation(wt[:, c, 0:D], w5[:, c, 0], ACT.Copy, scale=gb_s[:, c * SHIFTS, 0:1]).then_inc(scaled, 1)
            act.wait_ge(consts, N_CONST)
            a_.copy(identr[:], ident[:]).then_inc(hi_r, 1)
            act.wait_ge(s_small, 16 * 8)
            a_.copy(wr_hi[:], wr_raw[:, 0]).then_inc(hi_r, 1)
            a_.copy(wr_2[:], wr_raw[:, 1]).then_inc(hi_r, 1)

            def square(t, b):
                act.wait_ge(x_used, t + 1)
                a_.activation(xbuf[:, b], xbuf[:, b], ACT.Square).then_inc(sq_ready, 1)

            def flat(w, e):
                return w[:, bass.ds(e, 1)].rearrange("p e f -> p (e f)")

            def split_2(e):
                a_.copy(w2s[:, bass.ds(e, 1), :, 0].rearrange("p e c d -> p (e c) d"), raw_2[:]).then_inc(hi_2, 1)

            def high_rows(g, par):
                act.wait_ge(xn_ready, GT * g + GT)
                a_.copy(rows[:, par, :, 0:P], xn[:, :, 0:P])
                a_.copy(rows[:, par, :, TAIL:ROW], xn[:, :, P:D]).then_inc(row_hi, 1)

            def finish(g, par):
                for k in range(GT):
                    act.wait_ge(xt_ready, GT * g + k + 1)
                    a_.copy(xts[k], p_xt[k][:]).then_inc(xts_ready, 1)
                act.wait_ge(row_lo, g + 1)
                act.dma_start(xrow_d[:].rearrange("(t p) c -> p t c", p=P)[:, bass.ds(GT * g, GT)],
                              rows[:, par, :, 0:ROW].bitcast(F32))\
                    .then_inc(rows_stored[par], 16)
                act.dma_start(resid_d[:].rearrange("(t p) c -> p t c", p=P)[:, bass.ds(GT * g, GT)], h[:, par])\
                    .then_inc(rows_stored[par], 16)

            def group(g, par):
                if not early(g, 1):
                    square(GT * g - 1, (GT * par - 1) % 4)
                if not early(g, 2):
                    high_rows(g - 2, par)
                act.wait_ge(raw_a_loaded, 16 * g + 16)
                if early(g, 1):
                    act.wait_ge(row_sums, 1)
                    act.wait_ge(dset, N_SET)
                act.nop(nofuse=True)
                a_.copy(flat(w1_hi, g), raw_a[:]).then_inc(hi_a, 1)
                square(GT * g, GT * par)
                if not early(g, 2):
                    finish(g - 2, par)
                act.wait_ge(raw_b_loaded, 32 * g + 32)
                act.nop(nofuse=True)
                a_.copy(flat(w1_2, g), raw_b[:]).then_inc(hi_b, 1)
                if not early(g, 2):
                    act.wait_ge(raw_2_loaded, 16 * g - 16)
                    act.nop(nofuse=True)
                    split_2(g - 2)

            groups(act, group)
            square(TILES - 1, 3)
            high_rows(GROUPS - 2, 0)
            finish(GROUPS - 2, 0)
            act.wait_ge(raw_2_loaded, 16 * (NE - LATE) + 16)
            act.wait_ge(x_used, TILES)
            split_2(NE - LATE)
            high_rows(GROUPS - 1, 1)
            act.wait_ge(s_b1, 16)
            a_.copy(b1_hi.bitcast(F32R), b1_s).then_inc(b1_half, 1)
            finish(GROUPS - 1, 1)
            act.wait_ge(raw_2_loaded, 16 * NE)
            split_2(NE - 1)
            act.wait_ge(top_ready, 1)
            a_.activation(wex[:, 1], wex[:, 0], ACT.Exp).then_inc(exp_ready, 1)
            act.wait_ge(tile_ready, 1)
            a_.activation(part[:, :, 0], in_tile[:], ACT.Copy, scale=p_plus1[:, 0:1]).then_inc(part_ready, 1)

            def rows_t(j, k):
                act.wait_ge(gx_ready, j + 1)
                a_.copy(xts[k], p_x[:]).then_inc(gxs_ready, 1)

            def relu(j):
                act.wait_ge(ha_ready, j + 1)
                a_.activation(h_hi[:, 0:HA], p_ha[:], ACT.Relu).then_inc(relu_hi, 1)
                act.wait_ge(hb_ready, j + 1)
                a_.activation(h_hi[:, HA:FF], p_hb[:, 0:FF - HA], ACT.Relu).then_inc(relu_hi, 1)

            def tile(j, k, more, more2):
                act.wait_ge(thi_ready, 2 * j + 1)
                a_.copy(ht_hi[:, 0:4], p_hia[:].rearrange("p (c t) -> p c t", t=P)).then_inc(thi_copied, 1)
                act.wait_ge(thi_ready, 2 * j + 2)
                a_.copy(ht_hi[:, 4:6], p_hib[:, 0:2 * P].rearrange("p (c t) -> p c t", t=P)).then_inc(thi_copied, 1)
                if more:
                    relu(j + 1)
                if more2:
                    rows_t(j + 2, (k + 2) % UNROLL)

            rows_t(0, 0)
            rows_t(1, 1)
            relu(0)
            with act.Fori(0, SLOT_TILES - 2 * UNROLL + 1, UNROLL) as i:
                for k in range(UNROLL):
                    tile(i + k, k, True, True)
            for k in range(UNROLL):
                tile(SLOT_TILES - UNROLL + k, k, k < 2, k < 1)

        @block.vector
        def _(dve):
            v_ = nc.vector
            v_.memset(xbuf[D2:P, :, KCH - 1], 0.0).then_inc(lg_copied, 1)
            v_.memset(small[:], 1.0).then_inc(lo_2, 1)
            for k in range(2):
                v_.memset(bst[:, k], 0.0).then_inc(rows_stored[k], 1)
            dve.wait_ge(s_gb, 16)
            n = 0
            for c0 in range(0, CORE_CH, 2):
                for sh in range(1, SHIFTS):
                    for c in (c0, c0 + 1):
                        if sh == 1:
                            dve.wait_ge(scaled, c + 1)
                        else:
                            dve.wait_ge(dset, n - 1)
                        v_.scalar_tensor_tensor(out=wt[:, c, 0:D], in0=w5[:, c, sh], scalar=gb_s[:, c * SHIFTS + sh, 0:1],
                                                in1=wt[:, c, 0:D], op0=ALU.mult, op1=ALU.add).then_inc(dset, 1)
                        n += 1
            dve.wait_ge(s_w5[CORE_CH], 32)
            for k, rows_ in enumerate((P, HALO_B)):
                v_.tensor_scalar(wt[0:rows_, CORE_CH + k, 0:D], w5h[0:rows_, k],
                                 gb_s[0:rows_, CORE_CH * SHIFTS + k, 0:1], None, ALU.mult).then_inc(dset, 1)
            dve.wait_ge(s_small, 16 * 8)
            v_.tensor_copy(wt[:, :, D], cnt_s[:]).then_inc(dset, 1)
            dve.wait_ge(row_sums, 1)
            v_.tensor_copy(cb_row[:], p_set[0:2, 0:D]).then_inc(row_copied, 1)
            dve.wait_ge(hi_r, 3)
            v_.tensor_tensor(wr_lo[:], wr_raw[:, 0], wr_hi[:].bitcast(F32), ALU.subtract)
            v_.tensor_tensor(wr_b[:], wr_raw[0:D2, 1], wr_2[0:D2].bitcast(F32), ALU.subtract).then_inc(wr_split, 1)
            dve.wait_ge(bc_ready, 1)
            v_.tensor_copy(cb[:], p_bc[:, 0:2 * D].rearrange("p (n d) -> p n d", n=2)).then_inc(cb_ready, 1)
            dve.wait_ge(cb_ready, 1)

            def copy_logits(g):
                dve.wait_ge(lg_ready, g + 1)
                v_.tensor_scalar(logits[:, bass.ds(GT * g, GT)], p_lg[:, 0:GT * NE].rearrange("p (t e) -> p t e", t=GT),
                                 1.0, None, ALU.mult).then_inc(lg_copied, 1)

            def low_2(e):
                dve.wait_ge(hi_2, e + 1)
                v_.tensor_tensor(w2s[:, bass.ds(e, 1), :, 1].rearrange("p e c d -> p (e c) d"), raw_2[:],
                                 w2s[:, bass.ds(e, 1), :, 0].rearrange("p e c d -> p (e c) d").bitcast(F32),
                                 ALU.subtract).then_inc(lo_2, 1)

            nmu, a, mu2, var, rstd, vln, rln = (small[:, n] for n in range(7))

            def moments(g, par):
                s0 = STEPS * g
                tok = p_tok[par][:].rearrange("p (k c) -> p k c", k=GT)
                dve.wait_ge(sq_used, GT * g + GT)
                v_.tensor_scalar(nmu, tok[:, :, D], -1.0 / FEAT, None, ALU.mult).then_inc(step, 1)
                v_.tensor_scalar(a, tok[:, :, D + 1], 1.0 / FEAT, EPS_TOK, ALU.mult, ALU.add).then_inc(step, 1)
                dve.wait_ge(step, s0 + 1)
                v_.tensor_tensor(mu2, nmu, nmu, ALU.mult).then_inc(step, 1)
                dve.wait_ge(step, s0 + 3)
                v_.tensor_tensor(var, a, mu2, ALU.subtract).then_inc(var_tok, 1)
                for k in range(GT):
                    v_.scalar_tensor_tensor(out=u[:, k], in0=cb[:, 0], scalar=nmu[:, k:k + 1], in1=tok[:, k, 0:D],
                                            op0=ALU.mult, op1=ALU.add).then_inc(step if k == 0 else p_free, 1)

            def hidden(g, par):
                s0 = STEPS * g
                dve.wait_ge(p_free, g + 1)
                dve.wait_ge(rstd_tok, g + 1)
                for k in range(GT):
                    v_.scalar_tensor_tensor(out=h[:, par, k], in0=u[:, k], scalar=rstd[:, k:k + 1], in1=cb[:, 1],
                                            op0=ALU.mult, op1=ALU.add).then_inc(step, 1)
                for k in range(GT):
                    dve.wait_ge(step, s0 + 5 + k)
                    v_.bn_stats(bst[:, k], h[:, par, k]).then_inc(step, 1)
                for k in range(GT):
                    dve.wait_ge(step, s0 + 7 + k)
                    dve.nop(nofuse=True)
                    v_.bn_aggr(mv[:, k], bst[:, k]).then_inc(step, 1)
                dve.wait_ge(step, s0 + 10)
                v_.tensor_scalar(vln, mv[:, :, 1], EPS_LN, None, ALU.add).then_inc(var_ln, 1)

            def normed(g, par):
                dve.wait_ge(rstd_ln, g + 1)
                for k in range(GT):
                    v_.tensor_scalar(xn[:, k], h[:, par, k], mv[:, k, 0:1], rln[:, k:k + 1],
                                     ALU.subtract, ALU.mult).then_inc(xn_ready, 1)

            def low_rows(g, par):
                dve.wait_ge(row_hi, g + 1)
                for o, lo, hi, high in ((P, 0, P, 0), (2 * P, P, D, TAIL)):
                    ins = v_.tensor_tensor(rows[:, par, :, o:o + hi - lo], xn[:, :, lo:hi],
                                           rows[:, par, :, high:high + hi - lo].bitcast(F32), ALU.subtract)
                ins.then_inc(row_lo, 1)

            def fold(t, b):
                dve.wait_ge(sq_ready, t + 1)
                half = CORE_CH // 2
                v_.tensor_tensor(xbuf[:, b, 0:half], xbuf[:, b, 0:half], xbuf[:, b, half:CORE_CH], ALU.add)\
                    .then_inc(sq_folded, 1)

            def group(g, par):
                if not early(g, 1):
                    fold(GT * g - 1, (GT * par - 1) % 4)
                if not early(g, 2):
                    low_rows(g - 2, par)
                if not early(g, 1):
                    moments(g - 1, 1 - par)
                fold(GT * g, GT * par)
                if not early(g, 1):
                    if not early(g, 3):
                        dve.wait_ge(rows_stored[1 - par], 16 * (g - 2 + par) + 1)
                    hidden(g - 1, 1 - par)
                if not early(g, 2):
                    low_2(g - 2)
                if not early(g, 1):
                    normed(g - 1, 1 - par)
                if not early(g, 2):
                    copy_logits(g - 2)

            groups(dve, group)
            fold(TILES - 1, 3)
            low_rows(GROUPS - 2, 0)
            moments(GROUPS - 1, 1)
            dve.wait_ge(rows_stored[1], ALL_STORED - 32)
            hidden(GROUPS - 1, 1)
            low_2(NE - LATE)
            normed(GROUPS - 1, 1)
            copy_logits(GROUPS - 2)
            low_rows(GROUPS - 1, 1)
            dve.wait_ge(b1_half, 1)
            v_.tensor_tensor(b1_s, b1_s, b1_hi, ALU.subtract).then_inc(b1_placed, 2)
            low_2(NE - 1)
            copy_logits(GROUPS - 1)
            dve.wait_ge(lg_copied, 1 + GROUPS)

            done = [0]

            def link(ins):
                done[0] += 1
                ins.then_inc(ds, 1)
                dve.wait_ge(ds, done[0])

            def over_e(x):
                return x.unsqueeze(1).to_broadcast((P, TILES, NE))

            def over_t(x):
                return x.unsqueeze(2).to_broadcast((P, TILES, NE))

            src = logits
            for k in range(TOPK):
                ohk = oh[:, k].rearrange("p e t -> p t e")
                link(v_.tensor_reduce(top[:, k], src[:], AX.X, ALU.max))
                link(v_.tensor_tensor(eq[:], src[:], over_t(top[:, k]), ALU.is_equal))
                link(v_.tensor_tensor(eq[:], eq[:], over_e(first_e[:]), ALU.mult))
                link(v_.tensor_reduce(found[:, k], eq[:], AX.X, ALU.max))
                link(v_.tensor_tensor(ohk, over_e(first_e[:]), over_t(found[:, k]), ALU.is_equal))
                if k == 0:
                    link(v_.scalar_tensor_tensor(out=l2[:], in0=ohk, scalar=-BIG, in1=src[:], op0=ALU.mult, op1=ALU.add))
                    src = l2
            v_.tensor_tensor(chosen[:], oh[:, 0], oh[:, 1], ALU.add).then_inc(chosen_ready, 1)
            v_.tensor_tensor(wex[:, 0], top[:, 1], top[:, 0], ALU.subtract).then_inc(top_ready, 1)

            dve.wait_ge(counts_ready, 1)
            link(v_.tensor_copy(tot[:].rearrange("p e t -> p (e t)"), p_disp[:, P:2 * P]))
            link(v_.tensor_tensor_scan(incl[:].rearrange("p e t -> p (e t)"), restart[:].rearrange("p e t -> p (e t)"),
                                       tot[:].rearrange("p e t -> p (e t)"), 0.0, ALU.mult, ALU.add))
            v_.memset(e_one[:], 1.0)
            link(v_.tensor_scalar(e_int[:], incl[:, :, TILES - 1], float(P - 1), None, ALU.add))
            link(v_.tensor_scalar(e_int[:], e_int[:], 7, None, ALU.arith_shift_right))
            link(v_.tensor_copy(e_til[:], e_int[:]))
            link(v_.tensor_tensor_scan(e_end[:], e_one[:], e_til[:], 0.0, ALU.mult, ALU.add))
            link(v_.tensor_tensor(e_til[:], e_end[:], e_til[:], ALU.subtract))
            link(v_.tensor_tensor(incl[:], incl[:], tot[:], ALU.subtract))
            link(v_.scalar_tensor_tensor(out=base[:], in0=e_til[:].unsqueeze(2).to_broadcast((P, NE, TILES)),
                                         scalar=float(P), in1=incl[:], op0=ALU.mult, op1=ALU.add))
            link(v_.tensor_tensor(base[:], base[:], p_disp[:, 0:P].rearrange("p (e t) -> p e t", e=NE), ALU.add))
            for k in range(TOPK):
                link(v_.tensor_tensor(picked[:, k], oh[:, k], base[:], ALU.mult))
            link(v_.tensor_reduce(slot_f[:, 0].rearrange("p (k t) -> p k t", k=TOPK),
                                  picked.rearrange("p k e t -> p k t e"), AX.X, ALU.add))
            link(v_.tensor_copy(slot[:], slot_f[:, 0]))
            link(v_.tensor_scalar(slot_i[:, 0], slot[:], 7, None, ALU.arith_shift_right))
            link(v_.tensor_scalar(slot_i[:, 1], slot[:], P - 1, None, ALU.bitwise_and))
            link(v_.tensor_copy(slot_f[:], slot_i[:]))
            NT = TOPK * TILES
            for k in range(2):
                dve.wait_ge(rows_stored[k], ALL_STORED)
            v_.tensor_tensor(in_tile[:], tile_no[:, 0:SLOT_TILES].unsqueeze(1).to_broadcast((P, NT, SLOT_TILES)),
                             slot_f[:, 0].unsqueeze(2).to_broadcast((P, NT, SLOT_TILES)), ALU.is_equal)\
                .then_inc(tile_ready, 1)
            for q in range(4):
                m = NT // 4
                v_.tensor_tensor(in_row[:, q * m:(q + 1) * m], row128[:].unsqueeze(1).to_broadcast((P, m, P)),
                                 slot_f[:, 1, q * m:(q + 1) * m].unsqueeze(2).to_broadcast((P, m, P)), ALU.is_equal)\
                    .then_inc(hot_ready, 1)
            T1 = SLOT_TILES + 1
            link(v_.tensor_tensor(e_cmp, tile_no[0:1].unsqueeze(2).to_broadcast((1, T1, NE)),
                                  e_end[0:1].unsqueeze(1).to_broadcast((1, T1, NE)), ALU.is_ge))
            link(v_.tensor_reduce(e_sum[:], e_cmp, AX.X, ALU.add))
            dve.wait_ge(tab_sums, 1)
            link(v_.tensor_copy(ts[:], p_disp[:, 0:2 * SLOT_TILES].rearrange("p (n a) -> p n a", n=2)))
            link(v_.scalar_tensor_tensor(out=code[:, 0], in0=ts[:, 1], scalar=float(P), in1=ts[:, 0],
                                         op0=ALU.mult, op1=ALU.add))
            link(v_.tensor_scalar(code[:, 1], ts[:, 0], 0.0, None, ALU.is_equal))
            link(v_.tensor_scalar(code_i[:], code[:, 0], -1.0, None, ALU.add))
            v_.tensor_scalar(tab[:, 0, 0:SLOT_TILES], code_i[:], N_TOK - 1, None, ALU.bitwise_and).then_inc(tab_ready, 1)
            link(v_.tensor_tensor(code[:, 2], code[:, 1], pad_row[:], ALU.mult))
            v_.scalar_tensor_tensor(out=tab[:, 1, UNROLL:UNROLL + SLOT_TILES], in0=code[:, 2], scalar=-1.0,
                                    in1=code[:, 0], op0=ALU.add, op1=ALU.add).then_inc(tab_ready, 1)
            v_.tensor_scalar(etab[:], e_sum[:], float(NE - 1), None, ALU.min).then_inc(etab_ready, 1)
            dve.wait_ge(exp_ready, 1)
            link(v_.tensor_scalar(wex[:, 2], wex[:, 1], 1.0, None, ALU.add))
            link(v_.reciprocal(wgt[:, 0], wex[:, 2]))
            v_.tensor_tensor(wgt[:, 1], wex[:, 1], wgt[:, 0], ALU.mult).then_inc(wgt_ready, 1)

            def low(j):
                for n, (lo, hi, src_) in enumerate(((0, HA, p_ha[:]), (HA, FF, p_hb[:, 0:FF - HA]))):
                    dve.wait_ge(relu_hi, 2 * j + n + 1)
                    v_.scalar_tensor_tensor(out=h_lo[:, lo:hi], in0=src_, scalar=0.0, in1=h_hi[:, lo:hi].bitcast(F32),
                                            op0=ALU.max, op1=ALU.subtract).then_inc(relu_lo, 1)

            def tile(j, k, more):
                for n, (lo, hi, src_) in enumerate(((0, 4, p_loa), (4, 6, p_lob))):
                    dve.wait_ge(tlo_ready, 2 * j + n + 1)
                    v_.tensor_copy(ht_lo[:, lo:hi], src_[:, 0:(hi - lo) * P].rearrange("p (c t) -> p c t", t=P))\
                        .then_inc(tlo_copied, 1)
                if more:
                    low(j + 1)
                e = dve.value_load(etab[0:1, bass.ds(j, 1)], min_val=0, max_val=NE - 1)
                dve.wait_ge(y_ready, j + 1)
                if not early(j, UNROLL):
                    dve.wait_ge(y_stored[k], (j - k) * 16 // UNROLL)
                v_.tensor_tensor(y_s[:, k], p_y[:, 0:D], b2_s[:, bass.ds(e, 1)].rearrange("p e d -> p (e d)"), ALU.add)\
                    .then_inc(y_half, 1)
                dve.wait_ge(y_half, j + 1)
                v_.tensor_tensor(y_s[:, k], y_s[:, k], p_y[:, D:2 * D], ALU.add).then_inc(y_copied, 1)

            low(0)
            dve.wait_ge(s_b2, 16)
            for k in range(UNROLL):
                tile(k, k, True)
            with dve.Fori(UNROLL, SLOT_TILES - 2 * UNROLL + 1, UNROLL) as i:
                for k in range(UNROLL):
                    tile(i + k, k, True)
            for k in range(UNROLL):
                tile(SLOT_TILES - UNROLL + k, k, k < 2)
            dve.wait_ge(res_loaded, 16)
            dve.wait_ge(wgt_ready, 1)
            n = TILES // FIN
            for c in range(FIN):
                dve.wait_ge(y_loaded[c], 32)
                for t in range(c * n, (c + 1) * n):
                    v_.scalar_tensor_tensor(out=res_f[:, t], in0=y0_f[:, t], scalar=wgt[:, 0, t:t + 1], in1=res_f[:, t],
                                            op0=ALU.mult, op1=ALU.add).then_inc(mixed, 1)
                for t in range(c * n, (c + 1) * n):
                    dve.wait_ge(mixed, t + 1)
                    ins = v_.scalar_tensor_tensor(out=res_f[:, t], in0=y1_f[:, t], scalar=wgt[:, 1, t:t + 1],
                                                  in1=res_f[:, t], op0=ALU.mult, op1=ALU.add)
                ins.then_inc(out_ready, 1)

        @block.tensor
        def _(pe):
            mm = nc.tensor.matmul
            pe.wait_ge(s_gb, 16)
            for c in range(CORE_CH):
                pe.wait_ge(s_w5[c], 16)
                for s in range(SHIFTS):
                    n = c * SHIFTS + s
                    mm(p_set[0:2, 0:D], gb_s[:, n], w5[:, c, s], start=(n == 0), stop=False)
            pe.wait_ge(s_w5[CORE_CH], 32)
            mm(p_set[0:2, 0:D], gb_s[:, N_W - 2], w5h[:, 0], start=False, stop=False)
            mm(p_set[0:2, 0:D], gb_s[0:HALO_B, N_W - 1], w5h[0:HALO_B, 1], start=False, stop=True).then_inc(row_sums, 1)
            pe.wait_ge(dset, N_SET)

            def spread():
                pe.wait_ge(s_small, 16 * 8)
                pe.wait_ge(consts, N_CONST)
                pe.wait_ge(row_copied, 1)
                mm(p_bc[:, 0:D], sel_s[:, 0], cb_row[:], start=True, stop=True)
                mm(p_bc[:, D:2 * D], sel_s[:, 1], cb_row[:], start=True, stop=False)
                mm(p_bc[:, D:2 * D], sel_s[:, 2], bias2_s[:], start=False, stop=False)
                mm(p_bc[:, D:2 * D], attn[:], proj_s[:, 0], start=False, stop=False)
                mm(p_bc[:, D:2 * D], attn[0:D2], proj_s[0:D2, 1], start=False, stop=True).then_inc(bc_ready, 1)

            def squares(t, b, o):
                pe.wait_ge(sq_folded, t + 1)
                for c in (*range(CORE_CH // 2), *range(CORE_CH, KCH)):
                    r = P if c < KCH - 1 else HALO_B
                    ins = mm(o[:, D + 1:D + 2], xbuf[0:r, b, c], wt[0:r, c, D:D + 1], start=(c == 0), stop=(c == KCH - 1))
                ins.then_inc(sq_used, 1)

            def embed(g, par):
                for k in range(GT):
                    t, b, o = GT * g + k, GT * par + k, p_tok[par][:, k * PC:(k + 1) * PC]
                    pe.wait_ge(x_loaded[b], 16 * (g - par) + 32)
                    if k == 0 and not early(g, 2):
                        pe.wait_ge(p_free, g - 1)
                    for c in range(KCH):
                        r = P if c < KCH - 1 else HALO_B
                        ins = mm(o[:, 0:D + 1], xbuf[0:r, b, c], wt[0:r, c, 0:D + 1], start=(c == 0), stop=(c == KCH - 1))
                    ins.then_inc(x_used, 1)
                    if early(t, 1):
                        spread()
                    if k == 1:
                        squares(t - 1, b - 1, p_tok[par][:, 0:PC])
                    elif not early(g, 1):
                        squares(t - 1, (b - 1) % 4, p_tok[1 - par][:, PC:2 * PC])
                    if k == 0 and not early(g, 2):
                        turn_rows(g - 2, par)

            def split_product(o, x, a, b, c, d):
                mm(o, x[:, 0:P], a, start=True, stop=False)
                mm(o, x[:, 0:P], b, start=False, stop=False)
                mm(o, x[:, P:2 * P], a, start=False, stop=False)
                mm(o, x[:, 2 * P:3 * P], c, start=False, stop=False)
                return mm(o, x[0:d.shape[0], 3 * P:4 * P], d, start=False, stop=True)

            def route(g):
                for k in range(GT):
                    pe.wait_ge(xts_ready, GT * g + k + 1)
                    if k == 0:
                        pe.wait_ge(wr_split, 1)
                        pe.wait_ge(lg_copied, g + 1)
                    ins = split_product(p_lg[:, k * NE:(k + 1) * NE], xts[k], wr_hi[:], wr_lo[:], wr_2[:], wr_b[:])
                ins.then_inc(lg_ready, 1)

            def turn(o, x):
                for q, at in enumerate((0, P, 2 * P, TAIL)):
                    ins = nc.tensor.transpose(o[:, q * P:(q + 1) * P].bitcast(F32R), x[:, at:at + P], identr[:])
                return ins

            def turn_rows(g, par):
                if isinstance(g, int):
                    pe.wait_ge(hi_r, 1)
                pe.wait_ge(row_lo, g + 1)
                for k in range(GT):
                    turn(p_xt[k], rows[:, par, k]).then_inc(xt_ready, 1)

            def group(g, par):
                embed(g, par)
                if not early(g, 2):
                    route(g - 2)

            groups(pe, group)
            squares(TILES - 1, 3, p_tok[1][:, PC:2 * PC])
            turn_rows(GROUPS - 2, 0)
            route(GROUPS - 2)
            turn_rows(GROUPS - 1, 1)
            route(GROUPS - 1)

            pe.wait_ge(chosen_ready, 1)
            ch = chosen[:].rearrange("p e t -> p (e t)")
            mm(p_disp[:, 0:P], tri[:], ch, start=True, stop=True)
            mm(p_disp[:, P:2 * P], onesb[:], ch, start=True, stop=True).then_inc(counts_ready, 1)
            NT = TOPK * TILES
            pe.wait_ge(part_ready, 2)
            for n in range(NT):
                if n % (NT // 4) == 0:
                    pe.wait_ge(hot_ready, n // (NT // 4) + 1)
                ins = mm(p_disp[:, 0:2 * SLOT_TILES], in_row[:, n], part[:, n].rearrange("p a b -> p (a b)"),
                         start=(n == 0), stop=(n == NT - 1))
            ins.then_inc(tab_sums, 1)

            def gathered(j, k):
                pe.wait_ge(g_loaded[k], 16 * (j - k) // UNROLL + 16)
                turn(p_x, gath[:, k]).then_inc(gx_ready, 1)

            def first_product(j, k):
                e = pe.value_load(etab[0:1, bass.ds(j, 1)], min_val=0, max_val=NE - 1)
                pe.wait_ge(gxs_ready, j + 1)
                for o, lo, hi, s in ((p_ha, 0, HA, ha_ready), (p_hb, HA, FF, hb_ready)):
                    a, b, c, d = (w[:, bass.ds(e, 1), lo:hi].rearrange("p e f -> p (e f)") for w in (w1_hi, w1_lo, w1_2, w1_b[0:D2 + 2]))
                    ins = split_product(o[:, 0:hi - lo], xts[k], a, b, c, d)
                    ins.then_inc(s, 1)
                return ins

            def turn_hidden(j):
                for n, (o, lo, hi) in enumerate(((p_hia, 0, 4), (p_hib, 4, 6))):
                    pe.wait_ge(relu_hi, 2 * j + n + 1)
                    for c in range(lo, hi):
                        ins = nc.tensor.transpose(o[:, (c - lo) * P:(c - lo + 1) * P].bitcast(F32R), h_hi[:, c * P:(c + 1) * P],
                                                  identr[:])
                    ins.then_inc(thi_ready, 1)
                for n, (o, lo, hi) in enumerate(((p_loa, 0, 4), (p_lob, 4, 6))):
                    pe.wait_ge(relu_lo, 2 * j + n + 1)
                    for c in range(lo, hi):
                        ins = nc.tensor.transpose(o[:, (c - lo) * P:(c - lo + 1) * P].bitcast(F32R), h_lo[:, c * P:(c + 1) * P],
                                                  identr[:])
                    ins.then_inc(tlo_ready, 1)

            def second_product(j):
                e = pe.value_load(etab[0:1, bass.ds(j, 1)], min_val=0, max_val=NE - 1)
                w = [w2s[:, bass.ds(e, 1), c].rearrange("p e n d -> p (e n d)") for c in range(FCH)]
                pe.wait_ge(thi_copied, 2 * j + 2)
                if not early(j, 1):
                    pe.wait_ge(y_copied, j)
                for c in range(FCH):
                    mm(p_y[:, 0:2 * D], ht_hi[:, c], w[c], start=(c == 0), stop=False)
                pe.wait_ge(tlo_copied, 2 * j + 2)
                for c in range(FCH):
                    ins = mm(p_y[:, 0:D], ht_lo[:, c], w[c][:, 0:D], start=False, stop=(c == FCH - 1))
                ins.then_inc(y_ready, 1)

            def tile(j, k, more, more2):
                if more:
                    ins = first_product(j + 1, (k + 1) % UNROLL)
                second_product(j)
                if more2:
                    gathered_next(j, k)
                if more:
                    turn_hidden(j + 1)

            def gathered_next(j, k):
                k2 = (k + 2) % UNROLL
                pe.wait_ge(g_loaded[k2], 16 * ((j - k) // UNROLL + (k + 2) // UNROLL) + 16)
                turn(p_x, gath[:, k2]).then_inc(gx_ready, 1)

            pe.wait_ge(etab_ready, 1)
            pe.wait_ge(ones_ready, 2)
            pe.wait_ge(g_loaded[0], 16)
            turn(p_x, gath[:, 0]).then_inc(gx_ready, 1)
            pe.wait_ge(lo_a, NE)
            pe.wait_ge(lo_b, NE)
            pe.wait_ge(lo_2, NE + 1)
            pe.wait_ge(b1_placed, 34)
            first_product(0, 0)
            pe.wait_ge(g_loaded[1], 16)
            turn(p_x, gath[:, 1]).then_inc(gx_ready, 1)
            turn_hidden(0)
            with pe.Fori(0, SLOT_TILES - 2 * UNROLL + 1, UNROLL) as i:
                for k in range(UNROLL):
                    tile(i + k, k, True, True)
            j = SLOT_TILES - UNROLL
            tile(j, 0, True, True)
            tile(j + 1, 1, True, False)
            tile(j + 2, 2, False, False)


def kernel(x, L0_tok_gamma, L0_tok_beta, L0_tok_W, L0_tok_b, L0_attn_proj_w, L0_attn_proj_b, L0_ffn_Wr, L0_ffn_W1,
           L0_ffn_b1, L0_ffn_W2, L0_ffn_b2):
    import concourse.bacc as bacc
    from concourse.bass_utils import run_bass_kernel_spmd

    x = np.asarray(x)
    patches = x.reshape(IMAGES, GRID, PATCH, GRID, PATCH, CH).transpose(0, 1, 3, 2, 4, 5)
    pad = np.zeros((IMAGES, SIDE + 2, SIDE + 2, CH), x.dtype)
    pad[:, 1:-1, 1:-1] = x
    lo, hi = slice(0, SIDE, PATCH), slice(PATCH + 1, SIDE + 2, PATCH)

    def across(a):
        return a.reshape(IMAGES, GRID, PATCH, GRID, CH).transpose(0, 1, 3, 2, 4).reshape(N_TOK, -1)

    def along(a):
        return a.reshape(IMAGES, GRID, GRID, PATCH, CH).reshape(N_TOK, -1)

    halo = np.concatenate([across(pad[:, 1:-1, lo]), across(pad[:, 1:-1, hi]),
                           along(pad[:, lo, 1:-1]), along(pad[:, hi, 1:-1])], axis=1)
    pix = np.concatenate([patches.reshape(N_TOK, CORE)[:, core_order()], halo], axis=1)
    pix = pix.reshape(TILES, P, CORE + HALO).transpose(0, 2, 1)
    full = (KCH - 1) * P
    pix_a = pix[:, :full].reshape(TILES, KCH - 1, P, P).transpose(0, 2, 1, 3)
    w_core, w_halo = by_slab(np.asarray(L0_tok_W))
    gb = np.stack([np.asarray(L0_tok_gamma), np.asarray(L0_tok_beta)], axis=1)
    g_core, g_halo = by_slab(gb)
    gb_s = np.zeros((P, N_W, 2), gb.dtype)
    gb_s[:, :CORE_CH * SHIFTS] = g_core.transpose(1, 0, 2, 3).reshape(P, -1, 2)
    gb_s[:, -2] = g_halo[:P]
    gb_s[:HALO_B, -1] = g_halo[P:]
    sel = np.zeros((2, 3, P), np.float32)
    sel[0, 0], sel[1, 1], sel[:, 2] = 1, 1, 1
    arrays = {
        "pix_a": pix_a, "pix_b": pix[:, full:], "w_core": w_core, "w_halo": w_halo, "gb": gb_s,
        "count": feature_maps()[2], "sel": sel,
        "bias2": np.stack([np.asarray(L0_tok_b), np.asarray(L0_attn_proj_b)]),
        "proj_t": np.asarray(L0_attn_proj_w).T, "wr": L0_ffn_Wr, "w1": L0_ffn_W1, "b1": L0_ffn_b1,
        "w2": L0_ffn_W2, "b2": L0_ffn_b2,
    }
    arrays = {n: np.ascontiguousarray(a) for n, a in arrays.items()}
    nc = bacc.Bacc("TRN2", target_bir_lowering=False, num_devices=1)
    args = [nc.dram_tensor(n, a.shape, mybir.dt.from_np(a.dtype), kind="ExternalInput").ap()
            for n, a in arrays.items()]
    args.append(nc.dram_tensor("out", (N_TOK, D), F32, kind="ExternalOutput").ap())
    vit_tower_kernel(nc, *args)
    r = run_bass_kernel_spmd(nc, [arrays], core_ids=[0])
    return r.results[0]["out"].reshape(IMAGES, GRID * GRID, D)
```

```python
from contextlib import ExitStack

import numpy as np
import concourse.bass as bass
from concourse import mybir

ALU = mybir.AluOpType
ACT = mybir.ActivationFunctionType
AX = mybir.AxisListType
F32 = mybir.dt.float32
F32R = mybir.dt.float32r
BF16 = mybir.dt.bfloat16
I32 = mybir.dt.int32
U32 = mybir.dt.uint32

P = 128
IMAGES, SIDE, CH = 32, 128, 3
PATCH = 16
GRID = SIDE // PATCH
SHIFTS = 5
D = 192
N_TOK = IMAGES * GRID * GRID
FEAT = PATCH * PATCH * SHIFTS * CH
CORE = PATCH * PATCH * CH
HALO = 4 * PATCH * CH
CORE_CH = CORE // P
KCH = CORE_CH + 2
HALO_B = HALO - P
N_W = CORE_CH * SHIFTS + 2
TILES = N_TOK // P
GT = 2
GROUPS = TILES // GT
EPS_TOK, EPS_LN = 1e-3, 1e-5
NE, TOPK = 8, 2
FF = 4 * D
FCH = FF // P
HA = 512
D2 = D - P
ROW = 2 * D
TAIL = ROW - D2
ROW_P = ROW + D2
SLOT_TILES = TOPK * N_TOK // P + NE - 1
UNROLL = 3
assert SLOT_TILES % (4 * UNROLL) == UNROLL
LATE = 2
PC = 256
BIG = 3e38


def core_order():
    edge = np.zeros((PATCH, PATCH, CH), int)
    edge[[0, -1]] += 1
    edge[:, [0, -1]] += 1
    kinds = [np.flatnonzero(edge.ravel() == n).reshape(-1, CORE_CH) for n in range(3)]
    return np.concatenate(kinds).T.ravel()


def feature_maps():
    def feat(i, j, s, c):
        return (i * PATCH + j) * SHIFTS * CH + s * CH + c

    core = np.full((CORE, SHIFTS), FEAT)
    for i in range(PATCH):
        for j in range(PATCH):
            shown = ((i, j), (i, j + 1), (i, j - 1), (i + 1, j), (i - 1, j))
            for s, (a, b) in enumerate(shown):
                if 0 <= a < PATCH and 0 <= b < PATCH:
                    for c in range(CH):
                        core[(i * PATCH + j) * CH + c, s] = feat(a, b, s, c)
    core = core[core_order()]
    last = PATCH - 1
    sides = [[feat(i, 0, 1, c) for i in range(PATCH) for c in range(CH)],
             [feat(i, last, 2, c) for i in range(PATCH) for c in range(CH)],
             [feat(0, j, 3, c) for j in range(PATCH) for c in range(CH)],
             [feat(last, j, 4, c) for j in range(PATCH) for c in range(CH)]]
    halo = np.concatenate(sides)
    count = np.concatenate([(core < FEAT).sum(1), np.ones(HALO), np.zeros(P - HALO_B)])
    return core, halo, count.reshape(KCH, P).T.astype(np.float32)


def by_slab(w):
    core, halo, _ = feature_maps()
    padded = np.concatenate([w, np.zeros((1, w.shape[1]), w.dtype)])
    return padded[core].reshape(CORE_CH, P, SHIFTS, -1), w[halo]



def vit_tower_kernel(nc, pix_a, pix_b, w_core, w_halo, gb, count, sel, bias2, proj_t, wr, w1, b1, w2,
                     b2, out):
    ctx = ExitStack()
    with ctx:
        def sem(name):
            return ctx.enter_context(nc.semaphore(name))

        def sb(name, shape, dt=F32, stack=ctx):
            return stack.enter_context(nc.sbuf_tensor(name, shape, dt))

        xrow_d = nc.dram_tensor("xrow_d", [N_TOK, ROW], F32)
        resid_d = nc.dram_tensor("resid_d", [N_TOK, D], F32)
        y_d = nc.dram_tensor("y_d", [TOPK * N_TOK + SLOT_TILES * P, D], F32)

        fin = ExitStack()
        res_f = sb("res_f", [P, TILES, D], stack=fin)
        y0_f = sb("y0_f", [P, TILES, D], stack=fin)
        y1_f = sb("y1_f", [P, TILES, D], stack=fin)
        fin.close()
        w1_hi = sb("w1_hi", [P, NE, FF], F32R)
        w1_lo = sb("w1_lo", [P, NE, FF], F32R)
        w1_2 = sb("w1_2", [P, NE, FF], F32R)
        setup = ExitStack()
        w5 = sb("w5", [P, CORE_CH, SHIFTS, D], stack=setup)
        w5h = sb("w5h", [P, 2, D], stack=setup)
        setup.close()
        w1_b = sb("w1_b", [P, NE, FF], F32R)
        pixels = ExitStack()
        sb("w2s_first", [P, NE - LATE, FCH, 2, D], F32R, stack=pixels)
        xbuf = sb("xbuf", [P, 4, KCH, P], stack=pixels)
        attn = sb("attn", [P, P], stack=pixels)
        proj_s = sb("proj_s", [P, 2, D], stack=pixels)
        pixels.close()
        w2s = sb("w2s", [P, NE, FCH, 2, D], F32R)

        identr = sb("identr", [P, P], F32R)
        xts = [sb(f"xts{k}", [P, 4 * P], F32R)[:] for k in range(GT)]
        logits = sb("logits", [P, TILES, NE])
        wgt = sb("wgt", [P, TOPK, TILES])
        tab = sb("tab", [P, 2, SLOT_TILES + UNROLL], I32)
        etab = sb("etab", [1, SLOT_TILES + 1], I32)
        tri = sb("tri", [P, P], BF16)
        onesb = sb("onesb", [P, P], BF16)
        less = sb("less", [P, P], BF16)
        row128 = sb("row128", [P, P], BF16)
        tile_no = sb("tile_no", [P, SLOT_TILES + 1])
        pad_row = sb("pad_row", [P, SLOT_TILES])
        first_e = sb("first_e", [P, NE])
        block_no = sb("block_no", [P, TOPK * TILES])
        p_plus1 = sb("p_plus1", [P, 1])
        restart = sb("restart", [P, NE, TILES])
        raws = ExitStack()
        raw_a = sb("raw_a", [P, FF], stack=raws)
        raw_b = sb("raw_b", [P, FF], stack=raws)
        raw_2 = sb("raw_2", [P, FCH, D], stack=raws)
        raws.close()
        h_hi = sb("h_hi", [P, FF], F32R)
        h_lo = sb("h_lo", [P, FF], F32R)
        ht_hi = sb("ht_hi", [P, FCH, P], F32R)
        sb("rest_of_raw_2", [P, FCH * D - FF])

        emb = ExitStack()
        wt = sb("wt", [P, KCH, D + 2], stack=emb)
        gb_s = sb("gb_s", [P, N_W, 2], stack=emb)
        cnt_s = sb("cnt_s", [P, KCH], stack=emb)
        cb = sb("cb", [P, 2, D], stack=emb)
        folded = sb("folded", [P, 2, P], stack=emb)
        rows = sb("rows", [P, 2, GT, ROW], F32R, stack=emb)
        first = ExitStack()
        sel_s = sb("sel_s", [2, 3, P], stack=first)
        bias2_s = sb("bias2_s", [2, D], stack=first)
        cb_row = sb("cb_row", [2, D], stack=first)
        ident = sb("ident", [P, P], stack=first)
        ints = sb("ints", [P, P], I32, stack=first)
        first.close()
        h = sb("h", [P, 2, GT, D], stack=emb)
        xn = sb("xn", [P, GT, D], stack=emb)
        u = xn
        small = sb("small", [P, 8, GT], stack=emb)
        bst = sb("bst", [P, GT, 6], stack=emb)
        mv = sb("mv", [P, GT, 2], stack=emb)
        minus_half = sb("minus_half", [P, GT], stack=emb)
        wr_raw = sb("wr_raw", [P, 2, NE], stack=emb)
        wr_1 = sb("wr_1", [P, 2 * NE], F32R, stack=emb)
        wr_2 = sb("wr_2", [P, 2 * NE], F32R, stack=emb)
        emb.close()

        disp = ExitStack()
        oh = sb("oh", [P, TOPK, NE, TILES], stack=disp)
        eq = sb("eq", [P, TILES, NE], stack=disp)
        l2 = sb("l2", [P, TILES, NE], stack=disp)
        top = sb("top", [P, TOPK, TILES], stack=disp)
        found = sb("found", [P, TOPK, TILES], stack=disp)
        chosen = sb("chosen", [P, NE, TILES], BF16, stack=disp)
        incl = sb("incl", [P, NE, TILES], stack=disp)
        base = sb("base", [P, NE, TILES], stack=disp)
        spare = raw_2[:].rearrange("p c d -> p (c d)")
        e_cmp = spare[0:1, 0:(SLOT_TILES + 1) * NE].rearrange("p (a e) -> p a e", e=NE)
        e_int = sb("e_int", [P, NE], I32, stack=disp)
        e_til = sb("e_til", [P, NE], stack=disp)
        e_end = sb("e_end", [P, NE], stack=disp)
        e_one = sb("e_one", [P, NE], stack=disp)
        slot = sb("slot", [P, TOPK * TILES], I32, stack=disp)
        slot_i = sb("slot_i", [P, 2, TOPK * TILES], I32, stack=disp)
        slot_f = sb("slot_f", [P, 2, TOPK * TILES], stack=disp)
        part = sb("part", [P, TOPK * TILES, 2, SLOT_TILES], BF16, stack=disp)
        in_tile = sb("in_tile", [P, TOPK * TILES, SLOT_TILES], BF16, stack=disp)
        in_row = sb("in_row", [P, TOPK * TILES, P], BF16, stack=disp)
        code = sb("code", [P, SLOT_TILES], stack=disp)
        code_i = sb("code_i", [P, SLOT_TILES], I32, stack=disp)
        e_sum = sb("e_sum", [1, SLOT_TILES + 1], stack=disp)
        wex = sb("wex", [P, 3, TILES], stack=disp)
        disp.close()

        b1_s, b1_hi = raw_a[0:NE], raw_b[0:NE]

        xts.append(sb("xts2", [P, 4 * P], F32R)[:])
        b2_s = sb("b2_s", [P, NE, D])
        gath = sb("gath", [P, UNROLL, ROW_P], F32R)
        ht_lo = sb("ht_lo", [P, FCH, P], F32R)
        y_s = sb("y_s", [P, UNROLL, D])
        idx = sb("idx", [P, 2, 2, UNROLL], U32)

        bank = [ctx.enter_context(nc.psum_tensor(f"bank{n}", [P, 512], F32)) for n in range(8)]
        p_tok = bank[0:2]
        p_xt = [bank[2], bank[3]]
        p_lg, p_set, p_bc, p_disp = bank[4], bank[5], bank[6], bank[7]
        p_ha, p_hb, p_hia, p_hib, p_loa, p_lob, p_y, p_x = bank

        s_gb = sem("s_gb")
        s_w5 = [sem(f"s_w5_{c}") for c in range(CORE_CH + 1)]
        s_small = sem("s_small")
        consts = sem("consts")
        int_made = sem("int_made")
        row_sums = sem("row_sums")
        row_copied = sem("row_copied")
        bc_ready = sem("bc_ready")
        cb_ready = sem("cb_ready")
        scaled = sem("scaled")
        dset = sem("dset")
        hi_r = sem("hi_r")
        wr_split = sem("wr_split")
        x_loaded = [sem(f"x_loaded{b}") for b in range(4)]
        x_used = sem("x_used")
        sq_ready = sem("sq_ready")
        sq_folded = sem("sq_folded")
        sq_used = sem("sq_used")
        p_free = sem("p_free")
        step = sem("step")
        var_tok = sem("var_tok")
        rstd_tok = sem("rstd_tok")
        var_ln = sem("var_ln")
        rstd_ln = sem("rstd_ln")
        xn_ready = sem("xn_ready")
        row_hi = sem("row_hi")
        row_lo = sem("row_lo")
        xt_ready = sem("xt_ready")
        xts_ready = sem("xts_ready")
        lg_ready = sem("lg_ready")
        lg_copied = sem("lg_copied")
        rows_stored = [sem(f"rows_stored{k}") for k in range(2)]
        raw_a_loaded = sem("raw_a_loaded")
        raw_b_loaded = sem("raw_b_loaded")
        raw_2_loaded = sem("raw_2_loaded")
        hi_a, hi_b, hi_2 = sem("hi_a"), sem("hi_b"), sem("hi_2")
        lo_a, lo_b = sem("lo_a"), sem("lo_b")
        lo_2 = sem("lo_2")
        s_b1 = sem("s_b1")
        b1_half = sem("b1_half")
        b1_placed = sem("b1_placed")
        ds = sem("ds")
        chosen_ready = sem("chosen_ready")
        counts_ready = sem("counts_ready")
        top_ready = sem("top_ready")
        exp_ready = sem("exp_ready")
        wgt_ready = sem("wgt_ready")
        tile_ready = sem("tile_ready")
        part_ready = sem("part_ready")
        hot_ready = sem("hot_ready")
        tab_sums = sem("tab_sums")
        tab_ready = sem("tab_ready")
        etab_ready = sem("etab_ready")
        s_b2 = sem("s_b2")
        idx_staged = sem("idx_staged")
        g_loaded = [sem(f"g_loaded{k}") for k in range(UNROLL)]
        ones_ready = sem("ones_ready")
        gx_ready = sem("gx_ready")
        gxs_ready = sem("gxs_ready")
        ha_ready, hb_ready = sem("ha_ready"), sem("hb_ready")
        relu_hi = sem("relu_hi")
        relu_lo = sem("relu_lo")
        thi_ready, tlo_ready = sem("thi_ready"), sem("tlo_ready")
        thi_copied, tlo_copied = sem("thi_copied"), sem("tlo_copied")
        y_ready = sem("y_ready")
        y_half = sem("y_half")
        y_copied = sem("y_copied")
        y_stored = [sem(f"y_stored{k}") for k in range(UNROLL)]
        FIN = TILES // 2
        BY_POOL = list(range(1, FIN - 1, 2))
        BY_DVE = [c for c in range(FIN) if c not in BY_POOL]
        res_loaded = sem("res_loaded")
        y0_loaded = [sem(f"y0_loaded{c}") for c in range(FIN)]
        y1_loaded = [sem(f"y1_loaded{c}") for c in range(FIN)]
        y0_weighted = sem("y0_weighted")
        mixed = sem("mixed")
        out_dve, out_pool = sem("out_dve"), sem("out_pool")
        stored = sem("stored")

        N_CONST = 11
        N_SET = (SHIFTS - 1) * CORE_CH + 3
        N_SMALL = 16 * 8
        STEPS = 10
        ALL_STORED = 1 + 32 * GROUPS // 2
        B1_DONE = 2 + 2 * 16

        block = ctx.enter_context(nc.Block())

        def early(g, n):
            return isinstance(g, int) and g < n

        def groups(eng, group, last=0):
            for g in range(2):
                group(g, g)
            with eng.Fori(2, GROUPS - last - 1, 2) as i:
                for par in range(2):
                    group(i + par, par)
            for g in range(GROUPS - last, GROUPS):
                group(g, g % 2)

        @block.sync
        def _(sp):
            sp.dma_start(gb_s[:], gb).then_inc(s_gb, 16)
            for c in range(CORE_CH):
                sp.dma_start(w5[:, c], w_core[c]).then_inc(s_w5[c], 16)
            sp.dma_start(w5h[:, 0], w_halo[0:P]).then_inc(s_w5[CORE_CH], 16)
            sp.dma_start(w5h[0:HALO_B, 1], w_halo[P:HALO]).then_inc(s_w5[CORE_CH], 16)
            sp.dma_start(cnt_s[:], count).then_inc(s_small, 16)
            sp.dma_start(sel_s[:], sel).then_inc(s_small, 16)
            sp.dma_start(bias2_s[:], bias2).then_inc(s_small, 16)
            sp.dma_start(proj_s[:, 0], proj_t[0:P]).then_inc(s_small, 16)
            sp.dma_start(proj_s[0:D2, 1], proj_t[P:D]).then_inc(s_small, 16)
            sp.dma_start(wr_raw[:, 0], wr[0:P]).then_inc(s_small, 16)
            sp.dma_start(wr_raw[0:D2, 1], wr[P:D]).then_inc(s_small, 16)
            sp.dma_start(wr_raw[D2:P, 1], wr[P:D]).then_inc(s_small, 16)

            def group(g, par):
                for k in range(GT):
                    t, b = GT * g + k, GT * par + k
                    if not early(g, 2):
                        sp.wait_ge(sq_used, t - 3)
                    sp.dma_start(xbuf[:, b, 0:KCH - 1], pix_a[bass.ds(t, 1)].rearrange("o p k t -> p (o k) t"))\
                        .then_inc(x_loaded[b], 16)
                    sp.dma_start(xbuf[0:HALO_B, b, KCH - 1], pix_b[bass.ds(t, 1)].rearrange("o p t -> p (o t)"))\
                        .then_inc(x_loaded[b], 16)
                if not early(g, 1):
                    sp.wait_ge(lo_a, g)
                sp.dma_start(raw_a[:], w1[bass.ds(g, 1), 0:P].rearrange("e p f -> p (e f)")).then_inc(raw_a_loaded, 16)
                if not early(g, 1):
                    sp.wait_ge(lo_b, g)
                for lo in (0, D2):
                    sp.dma_start(raw_b[lo:lo + D2], w1[bass.ds(g, 1), P:D].rearrange("e p f -> p (e f)"))\
                        .then_inc(raw_b_loaded, 16)
                if not early(g, 2):
                    sp.wait_ge(lo_2, g - 1)
                    sp.dma_start(raw_2[:], w2[bass.ds(g - 2, 1)].rearrange("e (c p) d -> p (e c) d", p=P))\
                        .then_inc(raw_2_loaded, 16)

            groups(sp, group)
            for e in range(NE - LATE, NE):
                sp.wait_ge(lo_2, e + 1)
                sp.dma_start(raw_2[:], w2[e].rearrange("(c p) d -> p c d", p=P)).then_inc(raw_2_loaded, 16)
                if e == NE - LATE:
                    sp.wait_ge(lo_a, NE)
                    sp.wait_ge(lo_b, NE)
                    sp.dma_start(b1_s, b1).then_inc(s_b1, 16)
            sp.wait_ge(b1_placed, 2)
            sp.dma_start(w1_b[D2:D2 + 1].bitcast(F32), b1_hi).then_inc(b1_placed, 16)
            sp.dma_start(w1_b[D2 + 1:D2 + 2].bitcast(F32), b1_s).then_inc(b1_placed, 16)
            sp.wait_ge(tab_ready, 2)
            sp.wait_ge(etab_ready, 1)
            sp.wait_ge(b1_placed, B1_DONE)
            sp.dma_start(b2_s[:].rearrange("p e d -> p (e d)"),
                         b2.rearrange("(o e) d -> o (e d)", o=1).to_broadcast((P, NE * D))).then_inc(s_b2, 16)
            sp.wait_ge(hb_ready, SLOT_TILES)
            for k in range(2):
                sp.wait_ge(rows_stored[k], ALL_STORED)
            sp.dma_start(res_f[:], resid_d[:].rearrange("(t p) d -> p t d", p=P)).then_inc(res_loaded, 16)
            for k in range(UNROLL):
                sp.wait_ge(y_stored[k], 16 * (SLOT_TILES // UNROLL))
            n = TILES // FIN
            for c in range(FIN):
                for k, buf, loaded in ((0, y0_f, y0_loaded), (1, y1_f, y1_loaded)):
                    at = k * N_TOK + c * n * P
                    sp.dma_start(buf[:, c * n:(c + 1) * n],
                                 y_d[at:at + n * P].rearrange("(t p) d -> p t d", p=P)).then_inc(loaded[c], 16)
            for c in range(FIN):
                if c in BY_POOL:
                    sp.wait_ge(out_pool, BY_POOL.index(c) + 1)
                else:
                    sp.wait_ge(out_dve, BY_DVE.index(c) + 1)
                sp.dma_start(out[c * n * P:(c + 1) * n * P].rearrange("(t p) d -> p t d", p=P),
                             res_f[:, c * n:(c + 1) * n]).then_inc(stored, 16)
            sp.wait_ge(stored, 16 * FIN)

        @block.gpsimd
        def _(pool):
            g_ = nc.gpsimd
            g_.memset(onesb[:], 1.0).then_inc(consts, 1)
            g_.memset(ident[:], 1.0).then_inc(consts, 1)
            g_.memset(tri[:], 1.0).then_inc(consts, 1)
            g_.memset(minus_half[:], -0.5).then_inc(consts, 1)
            g_.memset(less[:], -1.0).then_inc(consts, 1)
            g_.memset(restart[:], 1.0).then_inc(consts, 1)
            pool.wait_ge(consts, 6)
            g_.affine_select(out=ident[:], in_=ident[:], compare_op=ALU.is_equal, fill=0.0, base=0,
                             pattern=[[-1, P]], channel_multiplier=1).then_inc(consts, 1)
            g_.affine_select(out=tri[:], in_=tri[:], compare_op=ALU.is_gt, fill=0.0, base=0,
                             pattern=[[1, P]], channel_multiplier=-1).then_inc(consts, 1)
            g_.memset(restart[:, :, 0:1], 0.0).then_inc(consts, 1)

            def floats(out_, n, pattern, base_, cm):
                g_.iota(ints[:, 0:n], pattern=pattern, base=base_, channel_multiplier=cm).then_inc(int_made, 1)
                made[0] += 1
                pool.wait_ge(int_made, made[0])
                g_.tensor_copy(out_, ints[:, 0:n]).then_inc(int_made, 1)
                made[0] += 1
                pool.wait_ge(int_made, made[0])

            made = [0]
            floats(first_e[:], NE, [[-1, NE]], NE, 0)
            floats(row128[:], P, [[1, P]], 0, 0)
            floats(tile_no[:], SLOT_TILES + 1, [[1, SLOT_TILES + 1]], 0, 0)
            floats(pad_row[:], SLOT_TILES, [[P, SLOT_TILES]], TOPK * N_TOK + 1, 1)
            floats(block_no[:], TOPK * TILES, [[P, TOPK * TILES]], 0, 0)
            floats(p_plus1[:], 1, [[0, 1]], 1, 1)
            g_.memset(attn[:], 0.0).then_inc(consts, 1)
            g_.memset(tab[:, 1, 0:UNROLL], 0).then_inc(consts, 1)

            def rsqrt(to, frm, signal):
                g_.tensor_tensor(small[:, to], small[:, frm], minus_half[:], ALU.pow).then_inc(signal, 1)

            def flat(w, e):
                return w[:, bass.ds(e, 1)].rearrange("p e f -> p (e f)")

            def group(g, par):
                if not early(g, 2):
                    pool.wait_ge(rstd_ln, g - 1)
                pool.wait_ge(hi_a, g + 1)
                pool.nop(nofuse=True)
                g_.tensor_tensor(flat(w1_lo, g), raw_a[:], flat(w1_hi, g).bitcast(F32), ALU.subtract).then_inc(lo_a, 1)
                pool.wait_ge(lo_a, g + 1)
                if not early(g, 1):
                    pool.wait_ge(var_tok, g)
                    rsqrt(4, 3, rstd_tok)
                    pool.wait_ge(rstd_tok, g)
                pool.wait_ge(hi_b, g + 1)
                pool.nop(nofuse=True)
                g_.tensor_tensor(flat(w1_b[0:D2], g), raw_b[0:D2], flat(w1_2[0:D2], g).bitcast(F32),
                                 ALU.subtract).then_inc(lo_b, 1)
                pool.wait_ge(lo_b, g + 1)
                if not early(g, 1):
                    pool.wait_ge(var_ln, g)
                    rsqrt(6, 5, rstd_ln)

            pool.wait_ge(consts, N_CONST)
            groups(pool, group)
            pool.wait_ge(rstd_ln, GROUPS - 1)
            pool.wait_ge(var_tok, GROUPS)
            rsqrt(4, 3, rstd_tok)
            pool.wait_ge(rstd_tok, GROUPS)
            pool.wait_ge(var_ln, GROUPS)
            rsqrt(6, 5, rstd_ln)
            pool.wait_ge(rstd_ln, GROUPS)
            pool.wait_ge(b1_half, 1)
            g_.tensor_tensor(b1_s, b1_s, b1_hi, ALU.subtract).then_inc(b1_placed, 2)
            pool.wait_ge(b1_placed, 2)
            pool.wait_ge(hi_2, NE)
            g_.tensor_tensor(w2s[:, NE - 1, :, 1], raw_2[:], w2s[:, NE - 1, :, 0].bitcast(F32), ALU.subtract)\
                .then_inc(lo_2, 1)

            NT = TOPK * TILES
            pool.wait_ge(lo_2, NE + 1)
            pool.wait_ge(tile_ready, 1)
            g_.tensor_tensor(part[:, :, 1], in_tile[:], block_no[:].unsqueeze(2).to_broadcast((P, NT, SLOT_TILES)),
                             ALU.mult).then_inc(part_ready, 1)

            def gather(k, ix):
                g_.indirect_dma_start(out=gath[:, k, 0:ROW].bitcast(F32), out_offset=None, in_=xrow_d[:],
                                      in_offset=bass.IndirectOffsetOnAxis(ap=ix, axis=0)).then_inc(g_loaded[k], 16)

            def scatter(k, ix):
                g_.indirect_dma_start(out=y_d[:], out_offset=bass.IndirectOffsetOnAxis(ap=ix, axis=0),
                                      in_=y_s[:, k], in_offset=None).then_inc(y_stored[k], 16)

            pool.wait_ge(tab_ready, 2)
            pool.wait_ge(etab_ready, 1)
            pool.wait_ge(b1_placed, B1_DONE)
            for k in range(2):
                pool.wait_ge(rows_stored[k], ALL_STORED)
            gather(0, tab[:, 0, 0:1].bitcast(U32))
            g_.memset(gath[:, :, ROW:ROW + 2].bitcast(F32), 1.0).then_inc(ones_ready, 1)
            g_.memset(gath[:, :, ROW + 2:ROW_P].bitcast(F32), 0.0).then_inc(ones_ready, 1)
            for k in range(1, UNROLL):
                gather(k, tab[:, 0, k:k + 1].bitcast(U32))

            def turn(j, par):
                g_.tensor_copy(idx[:, par].bitcast(I32), tab[:, :, bass.ds(j + UNROLL, UNROLL)]).then_inc(idx_staged, 1)
                for k in range(UNROLL):
                    pool.wait_ge(gx_ready, j + k + 1)
                    if k == 0:
                        pool.wait_ge(idx_staged, (j + UNROLL) // UNROLL if isinstance(j, int) else j // UNROLL + 1)
                    pool.nop(nofuse=True)
                    gather(k, idx[:, par, 0, k:k + 1])
                    pool.wait_ge(y_copied, j + k + 2)
                    pool.nop(nofuse=True)
                    scatter(k, idx[:, par, 1, k:k + 1])

            with pool.Fori(0, SLOT_TILES - 3 * UNROLL + 1, 2 * UNROLL) as i:
                for par in range(2):
                    turn(i + par * UNROLL, par)
            for k in range(UNROLL):
                j = SLOT_TILES - UNROLL + k
                pool.wait_ge(y_copied, j + 2)
                scatter(k, tab[:, 1, j + UNROLL:j + UNROLL + 1].bitcast(U32))
            n = TILES // FIN
            for m, c in enumerate(BY_POOL):
                pool.wait_ge(mixed, (c + 1) * n)
                pool.wait_ge(y0_weighted, c + 1)
                if m:
                    pool.wait_ge(out_pool, m)
                g_.tensor_tensor(res_f[:, c * n:(c + 1) * n], res_f[:, c * n:(c + 1) * n],
                                 y0_f[:, c * n:(c + 1) * n], ALU.add).then_inc(out_pool, 1)

        @block.scalar
        def _(act):
            a_ = nc.scalar
            act.wait_ge(s_gb, 16)
            for c in range(CORE_CH):
                act.wait_ge(s_w5[c], 16)
                a_.activation(wt[:, c, 0:D], w5[:, c, 0], ACT.Copy, scale=gb_s[:, c * SHIFTS, 0:1]).then_inc(scaled, 1)
            act.wait_ge(consts, N_CONST)
            a_.copy(identr[:], ident[:]).then_inc(hi_r, 1)
            act.wait_ge(s_small, N_SMALL)
            a_.copy(wr_1[:, 0:NE], wr_raw[:, 0]).then_inc(hi_r, 1)
            a_.copy(wr_2[:, 0:NE], wr_raw[:, 1]).then_inc(hi_r, 1)

            def square(t, b):
                act.wait_ge(x_used, t + 1)
                a_.activation(xbuf[:, b], xbuf[:, b], ACT.Square).then_inc(sq_ready, 1)

            def flat(w, e):
                return w[:, bass.ds(e, 1)].rearrange("p e f -> p (e f)")

            def split_2(e):
                a_.copy(w2s[:, bass.ds(e, 1), :, 0].rearrange("p e c d -> p (e c) d"), raw_2[:]).then_inc(hi_2, 1)

            def high_rows(g, par):
                act.wait_ge(xn_ready, GT * g + GT)
                a_.copy(rows[:, par, :, 0:P], xn[:, :, 0:P])
                a_.copy(rows[:, par, :, TAIL:ROW], xn[:, :, P:D]).then_inc(row_hi, 1)

            def finish(g, par):
                for k in range(GT):
                    act.wait_ge(xt_ready, GT * g + k + 1)
                    a_.copy(xts[k][:, 0:3 * P], p_xt[k][:, 0:3 * P]).then_inc(xts_ready, 1)
                act.wait_ge(row_lo, g + 1)
                act.dma_start(xrow_d[:].rearrange("(t p) c -> p t c", p=P)[:, bass.ds(GT * g, GT)],
                              rows[:, par].bitcast(F32))\
                    .then_inc(rows_stored[par], 16)
                act.dma_start(resid_d[:].rearrange("(t p) c -> p t c", p=P)[:, bass.ds(GT * g, GT)], h[:, par])\
                    .then_inc(rows_stored[par], 16)

            def group(g, par):
                if not early(g, 1):
                    square(GT * g - 1, (GT * par - 1) % 4)
                if not early(g, 2):
                    high_rows(g - 2, par)
                act.wait_ge(raw_a_loaded, 16 * g + 16)
                if early(g, 1):
                    act.wait_ge(row_sums, 1)
                    act.wait_ge(dset, N_SET)
                act.nop(nofuse=True)
                a_.copy(flat(w1_hi, g), raw_a[:]).then_inc(hi_a, 1)
                square(GT * g, GT * par)
                if not early(g, 2):
                    finish(g - 2, par)
                act.wait_ge(raw_b_loaded, 32 * g + 32)
                act.nop(nofuse=True)
                a_.copy(flat(w1_2, g), raw_b[:]).then_inc(hi_b, 1)
                if not early(g, 2):
                    act.wait_ge(raw_2_loaded, 16 * g - 16)
                    act.nop(nofuse=True)
                    split_2(g - 2)

            groups(act, group)
            square(TILES - 1, 3)
            high_rows(GROUPS - 2, 0)
            finish(GROUPS - 2, 0)
            high_rows(GROUPS - 1, 1)
            act.wait_ge(raw_2_loaded, 16 * (NE - LATE) + 16)
            act.wait_ge(x_used, TILES)
            split_2(NE - LATE)
            finish(GROUPS - 1, 1)
            act.wait_ge(s_b1, 16)
            a_.copy(b1_hi.bitcast(F32R), b1_s).then_inc(b1_half, 1)
            act.wait_ge(raw_2_loaded, 16 * NE)
            split_2(NE - 1)
            act.wait_ge(top_ready, 1)
            a_.activation(wex[:, 1], wex[:, 0], ACT.Exp).then_inc(exp_ready, 1)
            act.wait_ge(tile_ready, 1)
            a_.activation(part[:, :, 0], in_tile[:], ACT.Copy, scale=p_plus1[:, 0:1]).then_inc(part_ready, 1)

            def rows_t(j, k):
                act.wait_ge(gx_ready, j + 1)
                a_.copy(xts[k], p_x[:]).then_inc(gxs_ready, 1)

            def relu(j):
                act.wait_ge(ha_ready, j + 1)
                a_.activation(h_hi[:, 0:HA], p_ha[:], ACT.Relu).then_inc(relu_hi, 1)
                act.wait_ge(hb_ready, j + 1)
                a_.activation(h_hi[:, HA:FF], p_hb[:, 0:FF - HA], ACT.Relu).then_inc(relu_hi, 1)

            def tile(j, k, more, more2):
                act.wait_ge(thi_ready, 2 * j + 1)
                a_.copy(ht_hi[:, 0:4], p_hia[:].rearrange("p (c t) -> p c t", t=P)).then_inc(thi_copied, 1)
                act.wait_ge(thi_ready, 2 * j + 2)
                a_.copy(ht_hi[:, 4:6], p_hib[:, 0:2 * P].rearrange("p (c t) -> p c t", t=P)).then_inc(thi_copied, 1)
                if more:
                    relu(j + 1)
                if more2:
                    rows_t(j + 2, (k + 2) % UNROLL)

            rows_t(0, 0)
            relu(0)
            rows_t(1, 1)
            with act.Fori(0, SLOT_TILES - 2 * UNROLL + 1, UNROLL) as i:
                for k in range(UNROLL):
                    tile(i + k, k, True, True)
            for k in range(UNROLL):
                tile(SLOT_TILES - UNROLL + k, k, k < 2, k < 1)
            n = TILES // FIN
            act.wait_ge(wgt_ready, 1)
            for c in range(FIN):
                act.wait_ge(y0_loaded[c], 16)
                for t in range(c * n, (c + 1) * n):
                    ins = a_.activation(y0_f[:, t], y0_f[:, t], ACT.Copy, scale=wgt[:, 0, t:t + 1])
                ins.then_inc(y0_weighted, 1)

        @block.vector
        def _(dve):
            v_ = nc.vector
            v_.memset(xbuf[D2:P, :, KCH - 1], 0.0).then_inc(lg_copied, 1)
            v_.memset(small[:], 1.0).then_inc(lo_2, 1)
            for k in range(2):
                v_.memset(bst[:, k], 0.0).then_inc(rows_stored[k], 1)
            v_.memset(mv[:], 0.0).then_inc(y_copied, 1)
            dve.wait_ge(s_gb, 16)
            n = 0
            for c0 in range(0, CORE_CH, 2):
                for sh in range(1, SHIFTS):
                    for c in (c0, c0 + 1):
                        if sh == 1:
                            dve.wait_ge(scaled, c + 1)
                        else:
                            dve.wait_ge(dset, n - 1)
                        v_.scalar_tensor_tensor(out=wt[:, c, 0:D], in0=w5[:, c, sh], scalar=gb_s[:, c * SHIFTS + sh, 0:1],
                                                in1=wt[:, c, 0:D], op0=ALU.mult, op1=ALU.add).then_inc(dset, 1)
                        n += 1
            dve.wait_ge(s_w5[CORE_CH], 32)
            for k, rows_ in enumerate((P, HALO_B)):
                v_.tensor_scalar(wt[0:rows_, CORE_CH + k, 0:D], w5h[0:rows_, k],
                                 gb_s[0:rows_, CORE_CH * SHIFTS + k, 0:1], None, ALU.mult).then_inc(dset, 1)
            dve.wait_ge(s_small, N_SMALL)
            v_.tensor_copy(wt[:, :, D], cnt_s[:]).then_inc(dset, 1)
            dve.wait_ge(row_sums, 1)
            v_.tensor_copy(cb_row[:], p_set[0:2, 0:D]).then_inc(row_copied, 1)
            dve.wait_ge(hi_r, 3)
            v_.memset(wr_2[0:D2, NE:2 * NE].bitcast(F32), 0.0)
            v_.tensor_tensor(wr_1[:, NE:2 * NE], wr_raw[:, 0], wr_1[:, 0:NE].bitcast(F32), ALU.subtract)
            v_.tensor_tensor(wr_2[D2:P, NE:2 * NE], wr_raw[D2:P, 1], wr_2[D2:P, 0:NE].bitcast(F32), ALU.subtract)\
                .then_inc(wr_split, 1)
            dve.wait_ge(bc_ready, 1)
            v_.tensor_copy(cb[:], p_bc[:, 0:2 * D].rearrange("p (n d) -> p n d", n=2)).then_inc(cb_ready, 1)
            dve.wait_ge(cb_ready, 1)

            def copy_logits(g):
                dve.wait_ge(lg_ready, g + 1)
                lg = p_lg[:, 0:GT * 2 * NE].rearrange("p (t n e) -> p t n e", t=GT, n=2)
                dve.nop(nofuse=True)
                v_.tensor_reduce(logits[:, bass.ds(GT * g, GT)], lg.rearrange("p t n e -> p t e n"), AX.X, ALU.add)\
                    .then_inc(lg_copied, 1)

            def low_2(e):
                dve.wait_ge(hi_2, e + 1)
                v_.tensor_tensor(w2s[:, bass.ds(e, 1), :, 1].rearrange("p e c d -> p (e c) d"), raw_2[:],
                                 w2s[:, bass.ds(e, 1), :, 0].rearrange("p e c d -> p (e c) d").bitcast(F32),
                                 ALU.subtract).then_inc(lo_2, 1)

            nmu, a, mu2, var, rstd, vln, rln = (small[:, n] for n in range(7))

            def moments(g, par):
                s0 = STEPS * g
                tok = p_tok[par][:].rearrange("p (k c) -> p k c", k=GT)
                dve.wait_ge(sq_used, GT * g + GT)
                v_.tensor_scalar(nmu, tok[:, :, D], -1.0 / FEAT, None, ALU.mult).then_inc(step, 1)
                v_.tensor_scalar(a, tok[:, :, D + 1], 1.0 / FEAT, EPS_TOK, ALU.mult, ALU.add).then_inc(step, 1)
                dve.wait_ge(step, s0 + 1)
                v_.tensor_tensor(mu2, nmu, nmu, ALU.mult).then_inc(step, 1)
                dve.wait_ge(step, s0 + 3)
                v_.tensor_tensor(var, a, mu2, ALU.subtract).then_inc(var_tok, 1)
                for k in range(GT):
                    v_.scalar_tensor_tensor(out=u[:, k], in0=cb[:, 0], scalar=nmu[:, k:k + 1], in1=tok[:, k, 0:D],
                                            op0=ALU.mult, op1=ALU.add).then_inc(step if k == 0 else p_free, 1)

            def hidden(g, par):
                s0 = STEPS * g
                dve.wait_ge(p_free, g + 1)
                dve.wait_ge(rstd_tok, g + 1)
                for k in range(GT):
                    v_.scalar_tensor_tensor(out=h[:, par, k], in0=u[:, k], scalar=rstd[:, k:k + 1], in1=cb[:, 1],
                                            op0=ALU.mult, op1=ALU.add).then_inc(step, 1)
                for k in range(GT):
                    dve.wait_ge(step, s0 + 5 + k)
                    v_.bn_stats(bst[:, k], h[:, par, k]).then_inc(step, 1)
                for k in range(GT):
                    dve.wait_ge(step, s0 + 7 + k)
                    dve.nop(nofuse=True)
                    v_.bn_aggr(mv[:, k], bst[:, k]).then_inc(step, 1)
                dve.wait_ge(step, s0 + 10)
                v_.tensor_scalar(vln, mv[:, :, 1], EPS_LN, None, ALU.add).then_inc(var_ln, 1)

            def normed(g, par):
                dve.wait_ge(rstd_ln, g + 1)
                for k in range(GT):
                    v_.tensor_scalar(xn[:, k], h[:, par, k], mv[:, k, 0:1], rln[:, k:k + 1],
                                     ALU.subtract, ALU.mult).then_inc(xn_ready, 1)

            def low_rows(g, par):
                dve.wait_ge(row_hi, g + 1)
                for o, lo, hi, high in ((P, 0, P, 0), (2 * P, P, D, TAIL)):
                    ins = v_.tensor_tensor(rows[:, par, :, o:o + hi - lo], xn[:, :, lo:hi],
                                           rows[:, par, :, high:high + hi - lo].bitcast(F32), ALU.subtract)
                ins.then_inc(row_lo, 1)

            def fold(t, b):
                dve.wait_ge(sq_ready, t + 1)
                v_.tensor_reduce(folded[:, b % 2], xbuf[:, b, 0:CORE_CH].rearrange("p c t -> p t c"), AX.X, ALU.add)\
                    .then_inc(sq_folded, 1)

            def group(g, par):
                if not early(g, 2):
                    low_rows(g - 2, par)
                if not early(g, 1):
                    moments(g - 1, 1 - par)
                fold(GT * g, GT * par)
                if not early(g, 1):
                    if not early(g, 3):
                        dve.wait_ge(rows_stored[1 - par], 16 * (g - 2 + par) + 1)
                    hidden(g - 1, 1 - par)
                final = isinstance(g, int) and g == GROUPS - 1
                if final:
                    fold(GT * g + 1, GT * par + 1)
                elif not early(g, 2):
                    low_2(g - 2)
                if not early(g, 1):
                    normed(g - 1, 1 - par)
                if not final:
                    fold(GT * g + 1, GT * par + 1)
                if not early(g, 2):
                    copy_logits(g - 2)

            groups(dve, group, 2)
            low_rows(GROUPS - 2, 0)
            moments(GROUPS - 1, 1)
            low_2(NE - LATE - 1)
            dve.wait_ge(rows_stored[1], ALL_STORED - 32)
            hidden(GROUPS - 1, 1)
            normed(GROUPS - 1, 1)
            copy_logits(GROUPS - 2)
            low_rows(GROUPS - 1, 1)
            low_2(NE - LATE)
            copy_logits(GROUPS - 1)
            dve.wait_ge(lg_copied, 1 + GROUPS)

            done = [0]

            def link(ins):
                done[0] += 1
                ins.then_inc(ds, 1)
                dve.wait_ge(ds, done[0])

            def over_e(x):
                return x.unsqueeze(1).to_broadcast((P, TILES, NE))

            def over_t(x):
                return x.unsqueeze(2).to_broadcast((P, TILES, NE))

            src = logits
            for k in range(TOPK):
                ohk = oh[:, k].rearrange("p e t -> p t e")
                link(v_.tensor_reduce(top[:, k], src[:], AX.X, ALU.max))
                link(v_.tensor_tensor(eq[:], src[:], over_t(top[:, k]), ALU.is_equal))
                link(v_.tensor_tensor(eq[:], eq[:], over_e(first_e[:]), ALU.mult))
                link(v_.tensor_reduce(found[:, k], eq[:], AX.X, ALU.max))
                link(v_.tensor_tensor(ohk, over_e(first_e[:]), over_t(found[:, k]), ALU.is_equal))
                if k == 0:
                    link(v_.scalar_tensor_tensor(out=l2[:], in0=ohk, scalar=-BIG, in1=src[:], op0=ALU.mult, op1=ALU.add))
                    src = l2
            v_.tensor_tensor(chosen[:], oh[:, 0], oh[:, 1], ALU.add).then_inc(chosen_ready, 1)
            v_.tensor_tensor(wex[:, 0], top[:, 1], top[:, 0], ALU.subtract).then_inc(top_ready, 1)

            dve.wait_ge(counts_ready, 1)
            link(v_.tensor_tensor_scan(incl[:].rearrange("p e t -> p (e t)"), restart[:].rearrange("p e t -> p (e t)"),
                                       p_disp[:, P:2 * P], 0.0, ALU.mult, ALU.add))
            v_.memset(e_one[:], 1.0)
            link(v_.tensor_scalar(e_int[:], incl[:, :, TILES - 1], float(P - 1), None, ALU.add))
            v_.tensor_tensor(base[:], incl[:], p_disp[:, 0:P].rearrange("p (e t) -> p e t", e=NE), ALU.add)
            link(v_.tensor_scalar(e_int[:], e_int[:], 7, None, ALU.arith_shift_right))
            link(v_.tensor_copy(e_til[:], e_int[:]))
            link(v_.tensor_tensor_scan(e_end[:], e_one[:], e_til[:], 0.0, ALU.mult, ALU.add))
            link(v_.tensor_tensor(e_til[:], e_end[:], e_til[:], ALU.subtract))
            link(v_.scalar_tensor_tensor(out=base[:], in0=e_til[:].unsqueeze(2).to_broadcast((P, NE, TILES)),
                                         scalar=float(P), in1=base[:], op0=ALU.mult, op1=ALU.add))
            link(v_.tensor_tensor(oh[:], oh[:], base[:].unsqueeze(1).to_broadcast((P, TOPK, NE, TILES)), ALU.mult))
            link(v_.tensor_reduce(slot_f[:, 0].rearrange("p (k t) -> p k t", k=TOPK),
                                  oh[:].rearrange("p k e t -> p k t e"), AX.X, ALU.add))
            link(v_.tensor_copy(slot[:], slot_f[:, 0]))
            link(v_.tensor_scalar(slot_i[:, 0], slot[:], 7, None, ALU.arith_shift_right))
            link(v_.tensor_scalar(slot_i[:, 1], slot[:], P - 1, None, ALU.bitwise_and))
            link(v_.tensor_copy(slot_f[:], slot_i[:]))
            NT = TOPK * TILES
            for k in range(2):
                dve.wait_ge(rows_stored[k], ALL_STORED)
            v_.tensor_tensor(in_tile[:], tile_no[:, 0:SLOT_TILES].unsqueeze(1).to_broadcast((P, NT, SLOT_TILES)),
                             slot_f[:, 0].unsqueeze(2).to_broadcast((P, NT, SLOT_TILES)), ALU.is_equal)\
                .then_inc(tile_ready, 1)
            for q in range(4):
                m = NT // 4
                v_.tensor_tensor(in_row[:, q * m:(q + 1) * m], row128[:].unsqueeze(1).to_broadcast((P, m, P)),
                                 slot_f[:, 1, q * m:(q + 1) * m].unsqueeze(2).to_broadcast((P, m, P)), ALU.is_equal)\
                    .then_inc(hot_ready, 1)
            T1 = SLOT_TILES + 1
            dve.wait_ge(lo_2, NE + 1)
            link(v_.tensor_tensor(e_cmp, tile_no[0:1].unsqueeze(2).to_broadcast((1, T1, NE)),
                                  e_end[0:1].unsqueeze(1).to_broadcast((1, T1, NE)), ALU.is_ge))
            link(v_.tensor_reduce(e_sum[:], e_cmp, AX.X, ALU.add))
            v_.tensor_scalar(etab[:], e_sum[:], float(NE - 1), None, ALU.min).then_inc(etab_ready, 1)
            dve.wait_ge(tab_sums, 1)
            slot_code = p_disp[:, 0:SLOT_TILES]
            v_.tensor_scalar(code_i[:], slot_code, -1.0, None, ALU.add)
            link(v_.scalar_tensor_tensor(out=code[:], in0=slot_code, scalar=0.0, in1=pad_row[:],
                                         op0=ALU.is_equal, op1=ALU.mult))
            v_.tensor_scalar(tab[:, 0, 0:SLOT_TILES], code_i[:], N_TOK - 1, None, ALU.bitwise_and).then_inc(tab_ready, 1)
            v_.scalar_tensor_tensor(out=tab[:, 1, UNROLL:UNROLL + SLOT_TILES], in0=code[:], scalar=-1.0,
                                    in1=slot_code, op0=ALU.add, op1=ALU.add).then_inc(tab_ready, 1)
            dve.wait_ge(exp_ready, 1)
            link(v_.tensor_scalar(wex[:, 2], wex[:, 1], 1.0, None, ALU.add))
            link(v_.reciprocal(wgt[:, 0], wex[:, 2]))
            v_.tensor_tensor(wgt[:, 1], wex[:, 1], wgt[:, 0], ALU.mult).then_inc(wgt_ready, 1)

            def low(j):
                for n, (lo, hi, src_) in enumerate(((0, HA, p_ha[:]), (HA, FF, p_hb[:, 0:FF - HA]))):
                    dve.wait_ge(relu_hi, 2 * j + n + 1)
                    v_.scalar_tensor_tensor(out=h_lo[:, lo:hi], in0=src_, scalar=0.0, in1=h_hi[:, lo:hi].bitcast(F32),
                                            op0=ALU.max, op1=ALU.subtract).then_inc(relu_lo, 1)

            def tile(j, k, more):
                for n, (lo, hi, src_) in enumerate(((0, 4, p_loa), (4, 6, p_lob))):
                    dve.wait_ge(tlo_ready, 2 * j + n + 1)
                    v_.tensor_copy(ht_lo[:, lo:hi], src_[:, 0:(hi - lo) * P].rearrange("p (c t) -> p c t", t=P))\
                        .then_inc(tlo_copied, 1)
                if more:
                    low(j + 1)
                e = dve.value_load(etab[0:1, bass.ds(j, 1)], min_val=0, max_val=NE - 1)
                dve.wait_ge(y_ready, j + 1)
                if not early(j, UNROLL):
                    dve.wait_ge(y_stored[k], (j - k) * 16 // UNROLL)
                v_.tensor_tensor(y_s[:, k], p_y[:, 0:D], b2_s[:, bass.ds(e, 1)].rearrange("p e d -> p (e d)"), ALU.add)\
                    .then_inc(y_half, 1)
                dve.wait_ge(y_half, j + 1)
                v_.tensor_tensor(y_s[:, k], y_s[:, k], p_y[:, D:2 * D], ALU.add).then_inc(y_copied, 1)

            low(0)
            dve.wait_ge(s_b2, 16)
            for k in range(UNROLL):
                tile(k, k, True)
            with dve.Fori(UNROLL, SLOT_TILES - 2 * UNROLL + 1, UNROLL) as i:
                for k in range(UNROLL):
                    tile(i + k, k, True)
            for k in range(UNROLL):
                tile(SLOT_TILES - UNROLL + k, k, k < 2)
            dve.wait_ge(res_loaded, 16)
            dve.wait_ge(wgt_ready, 1)
            n = TILES // FIN
            for c in range(FIN):
                dve.wait_ge(y1_loaded[c], 16)
                for t in range(c * n, (c + 1) * n):
                    v_.scalar_tensor_tensor(out=res_f[:, t], in0=y1_f[:, t], scalar=wgt[:, 1, t:t + 1], in1=res_f[:, t],
                                            op0=ALU.mult, op1=ALU.add).then_inc(mixed, 1)
                if c in BY_DVE:
                    dve.wait_ge(mixed, (c + 1) * n)
                    dve.wait_ge(y0_weighted, c + 1)
                    v_.tensor_tensor(res_f[:, c * n:(c + 1) * n], res_f[:, c * n:(c + 1) * n],
                                     y0_f[:, c * n:(c + 1) * n], ALU.add).then_inc(out_dve, 1)

        @block.tensor
        def _(pe):
            mm = nc.tensor.matmul

            def keep_clock(n):
                for _ in range(n):
                    mm(p_lg[:], onesb[:], onesb[:].unsqueeze(1).to_broadcast((P, 4, P)), start=True, stop=True)

            pe.wait_ge(consts, 1)
            keep_clock(8)
            pe.wait_ge(s_gb, 16)
            for c in range(CORE_CH):
                pe.wait_ge(s_w5[c], 16)
                for s in range(SHIFTS):
                    n = c * SHIFTS + s
                    mm(p_set[0:2, 0:D], gb_s[:, n], w5[:, c, s], start=(n == 0), stop=False)
            pe.wait_ge(s_w5[CORE_CH], 32)
            mm(p_set[0:2, 0:D], gb_s[:, N_W - 2], w5h[:, 0], start=False, stop=False)
            mm(p_set[0:2, 0:D], gb_s[0:HALO_B, N_W - 1], w5h[0:HALO_B, 1], start=False, stop=True).then_inc(row_sums, 1)
            pe.wait_ge(dset, N_SET)

            def spread():
                pe.wait_ge(s_small, N_SMALL)
                pe.wait_ge(consts, N_CONST)
                mm(p_bc[:, D:2 * D], sel_s[:, 2], bias2_s[:], start=True, stop=False)
                mm(p_bc[:, D:2 * D], attn[:], proj_s[:, 0], start=False, stop=False)
                mm(p_bc[:, D:2 * D], attn[0:D2], proj_s[0:D2, 1], start=False, stop=False)
                pe.wait_ge(row_copied, 1)
                mm(p_bc[:, D:2 * D], sel_s[:, 1], cb_row[:], start=False, stop=True)
                mm(p_bc[:, 0:D], sel_s[:, 0], cb_row[:], start=True, stop=True).then_inc(bc_ready, 1)

            def squares(t, b, o):
                pe.wait_ge(sq_folded, t + 1)
                mm(o[:, D + 1:D + 2], folded[:, b % 2], wt[:, 0, D:D + 1], start=True, stop=False)
                for c in range(CORE_CH, KCH):
                    r = P if c < KCH - 1 else HALO_B
                    ins = mm(o[:, D + 1:D + 2], xbuf[0:r, b, c], wt[0:r, c, D:D + 1], start=False, stop=(c == KCH - 1))
                ins.then_inc(sq_used, 1)

            def embed(g, par):
                for k in range(GT):
                    t, b, o = GT * g + k, GT * par + k, p_tok[par][:, k * PC:(k + 1) * PC]
                    pe.wait_ge(x_loaded[b], 16 * (g - par) + 32)
                    if k == 0 and not early(g, 2):
                        pe.wait_ge(p_free, g - 1)
                    for c in range(KCH):
                        r = P if c < KCH - 1 else HALO_B
                        ins = mm(o[:, 0:D + 1], xbuf[0:r, b, c], wt[0:r, c, 0:D + 1], start=(c == 0), stop=(c == KCH - 1))
                    ins.then_inc(x_used, 1)
                    if early(t, 1):
                        spread()
                    if k == 1:
                        squares(t - 1, b - 1, p_tok[par][:, 0:PC])
                    elif not early(g, 1):
                        squares(t - 1, (b - 1) % 4, p_tok[1 - par][:, PC:2 * PC])
                    if k == 0 and not early(g, 2):
                        turn_rows(g - 2, par)

            def split_product(o, x, a, b, c, d):
                mm(o, x[:, 0:P], a, start=True, stop=False)
                mm(o, x[:, 0:P], b, start=False, stop=False)
                mm(o, x[:, P:2 * P], a, start=False, stop=False)
                mm(o, x[:, 2 * P:3 * P], c, start=False, stop=False)
                return mm(o, x[0:d.shape[0], 3 * P:4 * P], d, start=False, stop=True)

            def route(g):
                for k in range(GT):
                    pe.wait_ge(xts_ready, GT * g + k + 1)
                    if k == 0:
                        pe.wait_ge(wr_split, 1)
                        pe.wait_ge(lg_copied, g + 1)
                    x, o = xts[k], p_lg[:, k * 2 * NE:(k + 1) * 2 * NE]
                    mm(o, x[:, 0:P], wr_1[:], start=True, stop=False)
                    mm(o[:, 0:NE], x[:, P:2 * P], wr_1[:, 0:NE], start=False, stop=False)
                    ins = mm(o, x[:, 2 * P:3 * P], wr_2[:], start=False, stop=True)
                ins.then_inc(lg_ready, 1)

            def turn(o, x, starts=(0, P, 2 * P, TAIL)):
                for q, at in enumerate(starts):
                    ins = nc.tensor.transpose(o[:, q * P:(q + 1) * P].bitcast(F32R), x[:, at:at + P], identr[:])
                return ins

            def turn_rows(g, par):
                if isinstance(g, int):
                    pe.wait_ge(hi_r, 1)
                pe.wait_ge(row_lo, g + 1)
                for k in range(GT):
                    turn(p_xt[k], rows[:, par, k], (0, P, 2 * P)).then_inc(xt_ready, 1)

            def group(g, par):
                embed(g, par)
                if not early(g, 2):
                    route(g - 2)

            groups(pe, group)
            squares(TILES - 1, 3, p_tok[1][:, PC:2 * PC])
            turn_rows(GROUPS - 2, 0)
            route(GROUPS - 2)
            turn_rows(GROUPS - 1, 1)
            route(GROUPS - 1)

            pe.wait_ge(chosen_ready, 1)
            ch = chosen[:].rearrange("p e t -> p (e t)")
            mm(p_disp[:, 0:P], tri[:], ch, start=True, stop=False)
            mm(p_disp[:, 0:P], less[:], ch, start=False, stop=True)
            mm(p_disp[:, P:2 * P], onesb[:], ch, start=True, stop=True).then_inc(counts_ready, 1)
            NT = TOPK * TILES
            pe.wait_ge(part_ready, 2)
            for n in range(NT):
                if n % (NT // 4) == 0:
                    pe.wait_ge(hot_ready, n // (NT // 4) + 1)
                for m in range(2):
                    ins = mm(p_disp[:, 0:SLOT_TILES], in_row[:, n], part[:, n, m],
                             start=(n + m == 0), stop=(n + m == NT))
            ins.then_inc(tab_sums, 1)

            def expert_of(j):
                return pe.value_load(etab[0:1, bass.ds(j, 1)], min_val=0, max_val=NE - 1)

            def first_product(j, k, e):
                pe.wait_ge(gxs_ready, j + 1)
                for o, lo, hi, s in ((p_ha, 0, HA, ha_ready), (p_hb, HA, FF, hb_ready)):
                    a, b, c, d = (w[:, bass.ds(e, 1), lo:hi].rearrange("p e f -> p (e f)")
                                  for w in (w1_hi, w1_lo, w1_2, w1_b[0:D2 + 2]))
                    ins = split_product(o[:, 0:hi - lo], xts[k], a, b, c, d)
                    ins.then_inc(s, 1)
                return ins

            def turn_part(j, banks, x, split, turned):
                for n, (o, lo, hi) in enumerate(((banks[0], 0, 4), (banks[1], 4, 6))):
                    pe.wait_ge(split, 2 * j + n + 1)
                    for c in range(lo, hi):
                        ins = nc.tensor.transpose(o[:, (c - lo) * P:(c - lo + 1) * P].bitcast(F32R), x[:, c * P:(c + 1) * P],
                                                  identr[:])
                    ins.then_inc(turned, 1)

            def turn_high(j):
                turn_part(j, (p_hia, p_hib), h_hi, relu_hi, thi_ready)

            def turn_low(j):
                turn_part(j, (p_loa, p_lob), h_lo, relu_lo, tlo_ready)

            def second_weight(e, c):
                return w2s[:, bass.ds(e, 1), c].rearrange("p e n d -> p (e n d)")

            def second_product_high(j, e):
                pe.wait_ge(thi_copied, 2 * j + 2)
                pe.wait_ge(y_copied, j + 1)
                for c in range(FCH):
                    mm(p_y[:, 0:2 * D], ht_hi[:, c], second_weight(e, c), start=(c == 0), stop=False)

            def second_product_low(j, e):
                pe.wait_ge(tlo_copied, 2 * j + 2)
                for c in range(FCH):
                    ins = mm(p_y[:, 0:D], ht_lo[:, c], second_weight(e, c)[:, 0:D], start=False, stop=(c == FCH - 1))
                ins.then_inc(y_ready, 1)

            def tiles(j, n, last):
                e_next = expert_of(j + 1)
                for k in range(n):
                    left = n - 1 - k if last else n
                    if left:
                        first_product(j + k + 1, (k + 1) % UNROLL, e_next)
                    if k == 0:
                        e = expert_of(j)
                    second_product_high(j + k, e)
                    if left > 1:
                        gathered_next(j + k, k)
                    if left:
                        turn_high(j + k + 1)
                    second_product_low(j + k, e)
                    e = e_next
                    if left > 1 and k < n - 1:
                        e_next = expert_of(j + k + 2)
                    if left:
                        turn_low(j + k + 1)

            def gathered_next(j, k):
                k2 = (k + 2) % UNROLL
                pe.wait_ge(g_loaded[k2], 16 * ((j - k) // UNROLL + (k + 2) // UNROLL) + 16)
                turn(p_x, gath[:, k2]).then_inc(gx_ready, 1)

            pe.wait_ge(etab_ready, 1)
            keep_clock(12)
            pe.wait_ge(ones_ready, 2)
            pe.wait_ge(g_loaded[0], 16)
            turn(p_x, gath[:, 0]).then_inc(gx_ready, 1)
            pe.wait_ge(lo_a, NE)
            pe.wait_ge(lo_b, NE)
            pe.wait_ge(lo_2, NE + 1)
            pe.wait_ge(b1_placed, B1_DONE)
            first_product(0, 0, expert_of(0))
            pe.wait_ge(g_loaded[1], 16)
            turn(p_x, gath[:, 1]).then_inc(gx_ready, 1)
            turn_high(0)
            turn_low(0)
            with pe.Fori(0, SLOT_TILES - 5 * UNROLL + 1, 4 * UNROLL) as i:
                tiles(i, 4 * UNROLL, False)
            tiles(SLOT_TILES - UNROLL, UNROLL, True)


def kernel(x, L0_tok_gamma, L0_tok_beta, L0_tok_W, L0_tok_b, L0_attn_proj_w, L0_attn_proj_b, L0_ffn_Wr, L0_ffn_W1,
           L0_ffn_b1, L0_ffn_W2, L0_ffn_b2):
    import concourse.bacc as bacc
    from concourse.bass_utils import run_bass_kernel_spmd

    x = np.asarray(x)
    patches = x.reshape(IMAGES, GRID, PATCH, GRID, PATCH, CH).transpose(0, 1, 3, 2, 4, 5)
    pad = np.zeros((IMAGES, SIDE + 2, SIDE + 2, CH), x.dtype)
    pad[:, 1:-1, 1:-1] = x
    lo, hi = slice(0, SIDE, PATCH), slice(PATCH + 1, SIDE + 2, PATCH)

    def across(a):
        return a.reshape(IMAGES, GRID, PATCH, GRID, CH).transpose(0, 1, 3, 2, 4).reshape(N_TOK, -1)

    def along(a):
        return a.reshape(IMAGES, GRID, GRID, PATCH, CH).reshape(N_TOK, -1)

    halo = np.concatenate([across(pad[:, 1:-1, lo]), across(pad[:, 1:-1, hi]),
                           along(pad[:, lo, 1:-1]), along(pad[:, hi, 1:-1])], axis=1)
    pix = np.concatenate([patches.reshape(N_TOK, CORE)[:, core_order()], halo], axis=1)
    pix = pix.reshape(TILES, P, CORE + HALO).transpose(0, 2, 1)
    full = (KCH - 1) * P
    pix_a = pix[:, :full].reshape(TILES, KCH - 1, P, P).transpose(0, 2, 1, 3)
    w_core, w_halo = by_slab(np.asarray(L0_tok_W))
    gb = np.stack([np.asarray(L0_tok_gamma), np.asarray(L0_tok_beta)], axis=1)
    g_core, g_halo = by_slab(gb)
    gb_s = np.zeros((P, N_W, 2), gb.dtype)
    gb_s[:, :CORE_CH * SHIFTS] = g_core.transpose(1, 0, 2, 3).reshape(P, -1, 2)
    gb_s[:, -2] = g_halo[:P]
    gb_s[:HALO_B, -1] = g_halo[P:]
    sel = np.zeros((2, 3, P), np.float32)
    sel[0, 0], sel[1, 1], sel[:, 2] = 1, 1, 1
    arrays = {
        "pix_a": pix_a, "pix_b": pix[:, full:], "w_core": w_core, "w_halo": w_halo, "gb": gb_s,
        "count": feature_maps()[2], "sel": sel,
        "bias2": np.stack([np.asarray(L0_tok_b), np.asarray(L0_attn_proj_b)]),
        "proj_t": np.asarray(L0_attn_proj_w).T, "wr": L0_ffn_Wr, "w1": L0_ffn_W1, "b1": L0_ffn_b1,
        "w2": L0_ffn_W2, "b2": L0_ffn_b2,
    }
    arrays = {n: np.ascontiguousarray(a) for n, a in arrays.items()}
    nc = bacc.Bacc("TRN2", target_bir_lowering=False, num_devices=1)
    args = [nc.dram_tensor(n, a.shape, mybir.dt.from_np(a.dtype), kind="ExternalInput").ap()
            for n, a in arrays.items()]
    args.append(nc.dram_tensor("out", (N_TOK, D), F32, kind="ExternalOutput").ap())
    vit_tower_kernel(nc, *args)
    r = run_bass_kernel_spmd(nc, [arrays], core_ids=[0])
    return r.results[0]["out"].reshape(IMAGES, GRID * GRID, D)
```
